# Optimizing a Trainium2 kernel written in Bass

```python
import numpy as np
import jax
import jax.numpy as jnp

def _softmax(x, axis=-1):
    return jax.nn.softmax(x, axis=axis)

def _gelu(x):
    return jax.nn.gelu(x, approximate=True)

def _silu(x):
    return jax.nn.silu(x)

def _sigmoid(x):
    return jax.nn.sigmoid(x)

def _layernorm(x, axis=-1, eps=1e-05):
    m = jnp.mean(x, axis=axis, keepdims=True)
    v = jnp.var(x, axis=axis, keepdims=True)
    return (x - m) / jnp.sqrt(v + eps)

def _scatter_add(tgt, idx, src, axis=0):
    return tgt.at[idx].add(src)

def _segment_sum(src, seg, n):
    return jax.ops.segment_sum(src, seg, n)
kernel_name = 'mk_conv_preact_d2_conv_nchw512_r4_0ec2b3'

def setup_inputs(seed: int=0):
    np.random.seed(seed)
    _w = jnp.asarray

    def _rec_inputs():
        import jax
        import jax.numpy as jnp
        _gk = jax.random.key(seed)
        x = -0.0003929 + 0.9999 * jax.random.normal(jax.random.fold_in(_gk, 1), (8, 128, 16, 16), jnp.float32)
        return x
    x = _rec_inputs()

    def _L0_conv_setup():
        import jax, jax.numpy as jnp
        import numpy as np
        KERNEL = 3
        DILATIONS = (1, 2, 4, 8)
        NUM_HEADS = 8

        def _unfold3x3(x, dil):
            B, d, H, W = x.shape
            p = dil * (KERNEL - 1) // 2
            xp = jnp.pad(x, ((0, 0), (0, 0), (p, p), (p, p)))
            patches = [xp[:, :, i * dil:i * dil + H, j * dil:j * dil + W] for i in range(KERNEL) for j in range(KERNEL)]
            return jnp.stack(patches, axis=2)

        def _dilate_attention(q, k, v, dil, heads):
            B, d, H, W = q.shape
            hd = d // heads
            scale = hd ** (-0.5)
            N = H * W
            kk = KERNEL * KERNEL
            qh = q.reshape(B, heads, hd, N)
            kp = _unfold3x3(k, dil).reshape(B, heads, hd, kk, N)
            vp = _unfold3x3(v, dil).reshape(B, heads, hd, kk, N)
            attn = jnp.einsum('bhdn,bhdkn->bhnk', qh, kp) * scale
            attn = jax.nn.softmax(attn, axis=-1)
            out = jnp.einsum('bhnk,bhdkn->bnhd', attn, vp)
            return out.reshape(B, H, W, d)
        key = jax.random.key(seed)
        k1, k2, k3 = jax.random.split(key, 3)
        dim = 128
        B, H, W = (8, 16, 16)
        x = jax.random.normal(k1, (B, dim, H, W), dtype=jnp.float32)
        w_qkv = jax.random.normal(k2, (3 * dim, dim), dtype=jnp.float32) * dim ** (-0.5)
        w_gate = jax.random.normal(k3, (len(DILATIONS), dim), dtype=jnp.float32) * dim ** (-0.5)
        b_gate = jnp.zeros((len(DILATIONS),), dtype=jnp.float32)
        return {'x': x, 'w_qkv': w_qkv, 'w_gate': w_gate, 'b_gate': b_gate}
    _L0_conv_all = _L0_conv_setup()
    _L0_conv_in = {k: v for k, v in _L0_conv_all.items() if k in ('w_qkv', 'w_gate', 'b_gate')}
    del _L0_conv_all

    def _L1_conv_setup():
        import jax, jax.numpy as jnp
        import numpy as np
        INC = 128
        OUC = 128
        DIM_1H = 32
        NUM_HS = INC // DIM_1H
        key = jax.random.key(seed)
        k1, k2, k3, k4, k5 = jax.random.split(key, 5)
        embedx = jax.random.normal(k1, (16, INC, 16, 16), dtype=jnp.float32)
        W_qkv = jax.random.normal(k2, (OUC, INC), dtype=jnp.float32) * INC ** (-0.5)
        b_qkv = jax.random.normal(k3, (OUC,), dtype=jnp.float32) * 0.02
        W_proj = jax.random.normal(k4, (OUC, INC), dtype=jnp.float32) * INC ** (-0.5)
        b_proj = jax.random.normal(k5, (OUC,), dtype=jnp.float32) * 0.02
        return {'embedx': embedx, 'W_qkv': W_qkv, 'b_qkv': b_qkv, 'W_proj': W_proj, 'b_proj': b_proj}
    _L1_conv_all = _L1_conv_setup()
    _L1_conv_in = {k: v for k, v in _L1_conv_all.items() if k in ('W_qkv', 'b_qkv', 'W_proj', 'b_proj')}
    del _L1_conv_all
    return {'x': x, 'L0_conv_w_qkv': _L0_conv_in['w_qkv'], 'L0_conv_w_gate': _L0_conv_in['w_gate'], 'L0_conv_b_gate': _L0_conv_in['b_gate'], 'L1_conv_W_qkv': _L1_conv_in['W_qkv'], 'L1_conv_b_qkv': _L1_conv_in['b_qkv'], 'L1_conv_W_proj': _L1_conv_in['W_proj'], 'L1_conv_b_proj': _L1_conv_in['b_proj']}

def reference(x, L0_conv_w_qkv, L0_conv_w_gate, L0_conv_b_gate, L1_conv_W_qkv, L1_conv_b_qkv, L1_conv_W_proj, L1_conv_b_proj):
    import jax
    import jax.numpy as jnp

    def _L0_conv_ref(x, w_qkv, w_gate, b_gate):
        import jax, jax.numpy as jnp
        import numpy as np
        KERNEL = 3
        DILATIONS = (1, 2, 4, 8)
        NUM_HEADS = 8

        def _unfold3x3(x, dil):
            B, d, H, W = x.shape
            p = dil * (KERNEL - 1) // 2
            xp = jnp.pad(x, ((0, 0), (0, 0), (p, p), (p, p)))
            patches = [xp[:, :, i * dil:i * dil + H, j * dil:j * dil + W] for i in range(KERNEL) for j in range(KERNEL)]
            return jnp.stack(patches, axis=2)

        def _dilate_attention(q, k, v, dil, heads):
            B, d, H, W = q.shape
            hd = d // heads
            scale = hd ** (-0.5)
            N = H * W
            kk = KERNEL * KERNEL
            qh = q.reshape(B, heads, hd, N)
            kp = _unfold3x3(k, dil).reshape(B, heads, hd, kk, N)
            vp = _unfold3x3(v, dil).reshape(B, heads, hd, kk, N)
            attn = jnp.einsum('bhdn,bhdkn->bhnk', qh, kp) * scale
            attn = jax.nn.softmax(attn, axis=-1)
            out = jnp.einsum('bhnk,bhdkn->bnhd', attn, vp)
            return out.reshape(B, H, W, d)
        B, C, H, W = x.shape
        nd = len(DILATIONS)
        bd = C // nd
        hpb = NUM_HEADS // nd
        qkv = jnp.einsum('bchw,oc->bohw', x, w_qkv)
        qkv = qkv.reshape(B, 3, nd, bd, H, W)
        outs = []
        for i, dil in enumerate(DILATIONS):
            q, k, v = (qkv[:, 0, i], qkv[:, 1, i], qkv[:, 2, i])
            o = _dilate_attention(q, k, v, dil, hpb)
            outs.append(jnp.transpose(o, (0, 3, 1, 2)))
        pooled = x.mean(axis=(2, 3))
        gate = jax.nn.softmax(pooled @ w_gate.T + b_gate, axis=-1)
        out = jnp.concatenate([outs[i] * gate[:, i][:, None, None, None] for i in range(nd)], axis=1)
        return out

    def _L1_conv_ref(embedx, W_qkv, b_qkv, W_proj, b_proj):
        import jax, jax.numpy as jnp
        import numpy as np
        INC = 128
        OUC = 128
        DIM_1H = 32
        NUM_HS = INC // DIM_1H
        b, c, h, w = embedx.shape
        hw = h * w
        p = jnp.einsum('oc,bchw->bohw', W_qkv, embedx) + b_qkv[None, :, None, None]
        ph = p.reshape(b, NUM_HS, DIM_1H, hw)
        q = ph
        k = ph
        v = ph
        scale = hw ** (-0.5)
        att = jnp.einsum('bhdn,bhen->bhde', q, k) * scale
        att = jax.nn.softmax(att, axis=-1)
        out = jnp.einsum('bhde,bhen->bhdn', att, v).reshape(b, c, h, w)
        out = jnp.einsum('oc,bchw->bohw', W_proj, out) + b_proj[None, :, None, None]
        return out

    def _gn(v, G=32, eps=1e-05):
        B_, C_, H_, W_ = v.shape
        g = v.reshape(B_, G, C_ // G, H_, W_)
        m = jnp.mean(g, axis=(2, 3, 4), keepdims=True)
        s = jnp.var(g, axis=(2, 3, 4), keepdims=True)
        return ((g - m) / jnp.sqrt(s + eps)).reshape(v.shape)

    def _ln_c(v, eps=1e-06):
        m = jnp.mean(v, axis=1, keepdims=True)
        s = jnp.var(v, axis=1, keepdims=True)
        return (v - m) / jnp.sqrt(s + eps)

    def _ln_t(v, eps=1e-05):
        m = jnp.mean(v, axis=-1, keepdims=True)
        s = jnp.var(v, axis=-1, keepdims=True)
        return (v - m) / jnp.sqrt(s + eps)

    def _to_tokens(v):
        B_, C_, H_, W_ = v.shape
        return v.reshape(B_, C_, H_ * W_).transpose(0, 2, 1)

    def _from_tokens(t, like):
        B_, C_, H_, W_ = like.shape
        return t.transpose(0, 2, 1).reshape(B_, C_, H_, W_)
    x = x + _L0_conv_ref(_gn(x), L0_conv_w_qkv, L0_conv_w_gate, L0_conv_b_gate)
    x = x + _L1_conv_ref(_gn(x), L1_conv_W_qkv, L1_conv_b_qkv, L1_conv_W_proj, L1_conv_b_proj)
    return x

_drawn_inputs = setup_inputs


def setup_inputs(seed=0):
    import zlib

    import numpy as np

    out = dict(_drawn_inputs(seed))
    spreads = {'L0_conv_b_gate': (0.0, 0.543)}
    factors = {'L0_conv_w_gate': 8.0, 'L1_conv_b_qkv': 4.119, 'L1_conv_b_proj': 3.984}
    for name, (base, spread) in spreads.items():
        noise = np.random.default_rng([zlib.crc32(name.encode()), seed]).standard_normal(out[name].shape)
        drawn = base * np.exp(spread * noise) if base else spread * noise
        out[name] = jnp.asarray(drawn.astype(out[name].dtype))
    for name, factor in factors.items():
        out[name] = (out[name] * factor).astype(out[name].dtype)
    return out
```

```python
from contextlib import ExitStack

import concourse.bass as bass
from concourse import mybir

P = 128
B, H, W = 8, 16, 16
N = H * W
DIL = (1, 2, 4, 8)
ND = len(DIL)
CD = P // ND
HEADS = 2
HD = CD // HEADS
KK = 9
PHASES = 2
SLOTS = B // PHASES
QP = N // 4
QR = H // 4
GC = 4
H1 = 4
HD1 = P // H1
PAD = [d if d < 4 else 0 for d in DIL]
ROWS = [H + 2 * p for p in PAD]
EPS = 1e-5
ADDS = KK - 1
CENTRE_FIRST = (1, 0, 2)
SECOND_AFTER = (1, 2, 3, 5, 7, 8, 10)
SECOND_PE = ((0, 1), (2, 3), (4,), (5, 6))
SCALE0 = float(HD) ** -0.5
SCALE1 = float(N) ** -0.5

F32 = mybir.dt.float32
ALU = mybir.AluOpType
ACT = mybir.ActivationFunctionType
AX = mybir.AxisListType

W_QKV, W_GATE, W_1, W_1T, W_PT, W_B1, W_BP, W_B1R, W_BG, W_END = 0, 384, 388, 516, 644, 772, 773, 774, 902, 906
C_ID, C_GRP, C_RED, C_BLK, C_DIL, C_END = 0, 128, 256, 384, 512, 516


def columns(d, ci):
    co = (ci - 1) * d
    return max(0, -co), min(W, W - co), co


def pieces(s):
    d = DIL[s]
    if PAD[s]:
        return [(3, 0, 1, 0, 0, 0, d, H)]
    return [(1, 1, 0, 0, 0, 0, 0, H), (2, 0, 2, d, -d, 0, d, H - d)]


def row_offsets(s, j):
    if PAD[s]:
        return 0, 3
    return (0 if QR * j >= DIL[s] else 1), (3 if QR * j + DIL[s] < H else 2)


def valid_rows(s, ri):
    if PAD[s]:
        return 0, H
    ro = (ri - 1) * DIL[s]
    return max(0, -ro), min(H, H - ro)


def view(t, offset, dims):
    return bass.AP(t, offset, [[t[:].ap[0][0], P]] + [list(x) for x in dims if x[1] > 1])


def build(nc, x, wpack, consts, selc, out):
    with ExitStack() as ctx:
        def sb(name, shape):
            return ctx.enter_context(nc.sbuf_tensor(name, shape, F32))

        def sem(name):
            return ctx.enter_context(nc.semaphore(name))

        xt = sb("xt", [P, B, N])
        xn = sb("xn", [P, B, N])
        wp = sb("wp", [P, W_END])
        cs = sb("cs", [P, C_END])
        sel = sb("sel", [P, 4, ND, P])
        q = sb("q", [P, ND, PHASES, N])
        k = [sb(f"k{s}", [P, PHASES, ROWS[s], W]) for s in range(ND)]
        v = [sb(f"v{s}", [P, PHASES, ROWS[s], W]) for s in range(ND)]
        qk = [sb(f"qk{s}", [P, KK, N]) for s in range(ND)]
        pv = [sb(f"pv{s}", [P, KK, N]) for s in range(ND)]
        acc = sb("acc", [P, PHASES, ND, N])
        shifted = sb("shifted", [P, KK, QP])
        expd = sb("expd", [P, KK, QP])
        prob = sb("prob", [P, PHASES, KK, QP])
        smax = sb("smax", [P, QP])
        ssum = sb("ssum", [P, QP])
        srec = sb("srec", [P, QP])
        bst = sb("bst", [P, B, 6])
        mv = sb("mv", [P, B, 2])
        msq = sb("msq", [P, B])
        gst = sb("gst", [P, B, 2])
        gsq = sb("gsq", [P, B])
        gvar = sb("gvar", [P, B])
        mhalf = sb("mhalf", [P, B])
        rstd = sb("rstd", [P, B])
        nbias = sb("nbias", [P, B])
        pooled = sb("pooled", [P, B])
        pexp = sb("pexp", [P, PHASES, P])
        glog = sb("glog", [P, PHASES, ND])
        gsh = sb("gsh", [P, PHASES, ND])
        gex = sb("gex", [P, PHASES, ND])
        gpick = sb("gpick", [P, PHASES, ND])
        gmax = sb("gmax", [P, PHASES])
        gsum = sb("gsum", [P, PHASES])
        grec = sb("grec", [P, PHASES])
        gsel = sb("gsel", [P, PHASES])
        gate = sb("gate", [P, PHASES])
        x1 = sb("x1", [P, B, N])
        xn1 = sb("xn1", [P, SLOTS, N])
        pT = sb("pT", [P, SLOTS, 2, P])
        amax = sb("amax", [P, SLOTS])
        ash = sb("ash", [P, SLOTS, HD1])
        aex = sb("aex", [P, SLOTS, HD1])
        asum = sb("asum", [P, SLOTS])
        arec = sb("arec", [P, SLOTS])
        anorm = sb("anorm", [P, SLOTS, HD1])
        ablk = sb("ablk", [P, SLOTS, P])
        mT = sb("mT", [P, SLOTS, P])
        mwT = sb("mwT", [P, SLOTS, P])
        obias = sb("obias", [P, SLOTS])
        ot = sb("ot", [P, B, N])

        ps = ctx.enter_context(nc.psum_tensor("ps", [P, 8, 512], F32))
        SC = 4
        ST = 7
        LP, LS = 4, 6

        x_loaded = [sem(f"x_loaded{i}") for i in range(4)]
        w_loaded = sem("w_loaded")
        c_loaded = sem("c_loaded")
        sel_zeroed = sem("sel_zeroed")
        sel_loaded = sem("sel_loaded")
        halo_zeroed = sem("halo_zeroed")
        dve_settled = sem("dve_settled")
        mhalf_set = sem("mhalf_set")
        stats_ready = sem("stats_ready")
        gstats_ready = sem("gstats_ready")
        nbias_ready = sem("nbias_ready")
        var_ready = sem("var_ready")
        rstd_ready = sem("rstd_ready")
        xn_ready = sem("xn_ready")
        pexp_ready = sem("pexp_ready")
        glog_ready = sem("glog_ready")
        gshift_ready = sem("gshift_ready")
        gexp_ready = sem("gexp_ready")
        proj_ready = sem("proj_ready")
        proj_copied = sem("proj_copied")
        qk_ready = sem("qk_ready")
        scores_ready = sem("scores_ready")
        shift_ready = sem("shift_ready")
        exp_ready = sem("exp_ready")
        prob_ready = sem("prob_ready")
        spread_ready = sem("spread_ready")
        pv_ready = sem("pv_ready")
        added = sem("added")
        restored = sem("restored")
        obias_ready = sem("obias_ready")
        xn1_ready = sem("xn1_ready")
        pT_ready = sem("pT_ready")
        pT_copied = sem("pT_copied")
        att_ready = sem("att_ready")
        ashift_ready = sem("ashift_ready")
        aexp_ready = sem("aexp_ready")
        ablk_ready = sem("ablk_ready")
        mT_ready = sem("mT_ready")
        mT_copied = sem("mT_copied")
        mwT_ready = sem("mwT_ready")
        mwT_copied = sem("mwT_copied")
        fin_ready = sem("fin_ready")
        out_ready = sem("out_ready")
        out_stored = sem("out_stored")

        ident = cs[:, C_ID:C_ID + P]
        xph = xt[:].rearrange("p (j h) n -> p h j n", h=PHASES)
        x1ph = x1[:].rearrange("p (j h) n -> p h j n", h=PHASES)
        mvph = mv[:].rearrange("p (j h) t -> p h j t", h=PHASES)
        tiles = [(kind, s) for s in range(ND) for kind in (0, 1)] + [(2, s) for s in range(ND)]
        PROJ_BANKS = 6

        block = ctx.enter_context(nc.Block())

        @block.sync
        def _(sp):
            xv = x.rearrange("b c n -> c b n")
            for i in range(4):
                sp.dma_start(xt[:, 2 * i:2 * i + 2, :], xv[:, 2 * i:2 * i + 2, :]).then_inc(x_loaded[i], 16)
            sp.wait_ge(sel_zeroed, 1)
            for j in range(4):
                sp.dma_start(sel[32 * j:32 * j + 32, j, :, :], selc).then_inc(sel_loaded, 16)
            for n in range(B):
                b = PHASES * (n % SLOTS) + n // SLOTS
                sp.wait_ge(out_ready, n + 1)
                sp.dma_start(out[b], ot[:, b, :]).then_inc(out_stored, 16)
            sp.wait_ge(out_stored, 16 * B)

        @block.gpsimd
        def _(pool):
            nc.gpsimd.memset(mhalf[:], -0.5).then_inc(mhalf_set, 1)
            nc.gpsimd.memset(sel[:], 0.0).then_inc(sel_zeroed, 1)
            for s in range(ND):
                if PAD[s]:
                    for t in (k[s], v[s]):
                        for r in (0, PAD[s] + H):
                            last = nc.gpsimd.memset(t[:, :, r:r + PAD[s], :], 0.0)
            last.then_inc(halo_zeroed, 1)
            pool.wait_ge(var_ready, 1)
            pool.wait_ge(mhalf_set, 1)
            nc.gpsimd.tensor_tensor(rstd[:], gvar[:], mhalf[:], ALU.pow).then_inc(rstd_ready, 1)

            def rsqrt(g):
                bs = slice(g - 1, B, PHASES)
                pool.wait_ge(var_ready, g + 1)
                nc.gpsimd.tensor_tensor(rstd[:, bs], gvar[:, bs], mhalf[:, bs], ALU.pow).then_inc(rstd_ready, 1)

            def add(s, ph, n, slot, first=None):
                ci, ri = divmod(slot, 3)
                c0, c1, _ = columns(DIL[s], ci)
                r0, r1 = valid_rows(s, ri)

                def rect(t):
                    return t.rearrange("p (r c) -> p r c", c=W)[:, r0:r1, c0:c1]

                total = rect(acc[:, ph, s, :])
                if n:
                    pool.wait_ge(added, ADDS * (ND * ph + s) + n)
                src = total if first is None else rect(pv[s][:, first, :])
                nc.gpsimd.tensor_tensor(total, src, rect(pv[s][:, slot, :]), ALU.add).then_inc(added, 1)

            for ph in range(PHASES):
                for s in range(ND):
                    if ph == 1 and s == 1:
                        rsqrt(1)
                    n = 0
                    for part, ci in enumerate(CENTRE_FIRST):
                        pool.wait_ge(pv_ready, 12 * ph + 3 * s + part + 1)
                        for slot in (3 * ci, 3 * ci + 2) if ci == 1 else (3 * ci, 3 * ci + 1, 3 * ci + 2):
                            add(s, ph, n, slot, first=4 if n == 0 and PAD[s] else None)
                            n += 1
            rsqrt(2)

        @block.scalar
        def _(act):
            act.dma_start(wp[:], wpack).then_inc(w_loaded, 16)
            act.dma_start(cs[:], consts).then_inc(c_loaded, 16)
            act.wait_ge(halo_zeroed, 1)
            for n, (kind, s) in enumerate(tiles):
                act.wait_ge(proj_ready, n + 1)
                src = ps[:, n % PROJ_BANKS, :]
                if kind == 0:
                    nc.scalar.copy(q[:, s, :, :], src.rearrange("p (h n) -> p h n", h=PHASES)).then_inc(proj_copied, 1)
                else:
                    dst = (k, v)[kind - 1][s][:, :, PAD[s]:PAD[s] + H, :]
                    nc.scalar.copy(dst, src.rearrange("p (h r c) -> p h r c", h=PHASES, c=W)).then_inc(proj_copied, 1)
            act.wait_ge(gshift_ready, 1)
            nc.scalar.activation(gex[:], gsh[:], ACT.Exp).then_inc(gexp_ready, 1)
            for ph in range(PHASES):
                act.wait_ge(shift_ready, ph + 1)
                if ph:
                    act.wait_ge(prob_ready, ph)
                nc.scalar.activation(expd[:], shifted[:], ACT.Exp, scale=SCALE0).then_inc(exp_ready, 1)
            for ph in range(PHASES):
                act.wait_ge(nbias_ready, ph + 2)
                if ph:
                    act.wait_ge(fin_ready, SLOTS * ph)
                for j in range(SLOTS):
                    b = PHASES * j + ph
                    nc.scalar.activation(xn1[:, j, :], x1[:, b, :], ACT.Identity, bias=nbias[:, b:b + 1],
                                         scale=rstd[:, b:b + 1]).then_inc(xn1_ready, 1)
                act.wait_ge(ashift_ready, ph + 1)
                nc.scalar.activation(aex[:], ash[:], ACT.Exp, scale=SCALE1).then_inc(aexp_ready, 1)
                act.wait_ge(mT_ready, ph + 1)
                nc.scalar.copy(mT[:], ps[:, LS + 1, :].rearrange("p (j n) -> p j n", j=SLOTS)).then_inc(mT_copied, 1)
                act.wait_ge(mwT_ready, ph + 1)
                nc.scalar.copy(mwT[:], ps[:, LP, :].rearrange("p (j n) -> p j n", j=SLOTS)).then_inc(mwT_copied, 1)

        @block.vector
        def _(dve):
            settled = [0]

            def link(ins):
                settled[0] += 1
                ins.then_inc(dve_settled, 1)
                dve.wait_ge(dve_settled, settled[0])

            for s, d in enumerate(DIL):
                t = qk[s][:].rearrange("p (a i) (r c) -> p a (i r) c", i=3, c=W)
                nc.vector.memset(t[:, 0, :, 0:d], 0.0)
                last = nc.vector.memset(t[:, 2, :, W - d:W], 0.0)
            link(last)
            for s, d in enumerate(DIL):
                if not PAD[s]:
                    t = qk[s][:].rearrange("p (a i) n -> p a i n", i=3)
                    nc.vector.memset(t[:, :, 0, 0:d * W], 0.0)
                    last = nc.vector.memset(t[:, :, 2, (H - d) * W:N], 0.0)
            link(last)

            def channel_stats(src, b0s, g):
                for b in b0s:
                    if g == 0 and b % 2 == 0:
                        dve.wait_ge(x_loaded[b // 2], 16)
                    last = nc.vector.bn_stats(bst[:, b, :], src[:, b, :])
                link(last)
                for b in b0s:
                    last = nc.vector.bn_aggr(mv[:, b, :], bst[:, b, :])
                link(last)
                bs = slice(b0s[0], B, b0s[1] - b0s[0])
                link(nc.vector.tensor_tensor(msq[:, bs], mv[:, bs, 0], mv[:, bs, 0], ALU.mult))
                nc.vector.tensor_tensor(mv[:, bs, 1], mv[:, bs, 1], msq[:, bs], ALU.add).then_inc(stats_ready, 1)
                return bs

            def group_variance(bs, n, bank, g):
                dve.wait_ge(gstats_ready, g + 1)
                link(nc.vector.tensor_copy(gst[:, bs, :], ps[:, bank, 0:2 * n].rearrange("p (b t) -> p b t", t=2)))
                link(nc.vector.tensor_tensor(gsq[:, bs], gst[:, bs, 0], gst[:, bs, 0], ALU.mult))
                nc.vector.scalar_tensor_tensor(out=gvar[:, bs], in0=gst[:, bs, 1], scalar=EPS, in1=gsq[:, bs],
                                               op0=ALU.add, op1=ALU.subtract).then_inc(var_ready, 1)

            def norm_bias(bs, g):
                dve.wait_ge(rstd_ready, g + 1)
                nc.vector.scalar_tensor_tensor(out=nbias[:, bs], in0=gst[:, bs, 0], scalar=-1.0, in1=rstd[:, bs],
                                               op0=ALU.mult, op1=ALU.mult).then_inc(nbias_ready, 1)

            every = channel_stats(xt, range(B), 0)
            group_variance(every, B, ST, 0)
            norm_bias(every, 0)
            dve.wait_ge(nbias_ready, 1)
            for b in range(B):
                nc.vector.tensor_scalar(xn[:, b, :], xt[:, b, :], rstd[:, b:b + 1], nbias[:, b:b + 1],
                                        ALU.mult, ALU.add).then_inc(xn_ready, 1)
            link(nc.vector.tensor_tensor(pooled[:], mv[:, :, 0], rstd[:], ALU.mult))
            link(nc.vector.tensor_tensor(pooled[:], pooled[:], nbias[:], ALU.add))
            for ph in range(PHASES):
                dst = pexp[:, ph, :].rearrange("p (i j h) -> p i j h", j=SLOTS, h=HEADS)
                nc.vector.tensor_copy(dst, view(pooled, ph, [[0, P // (SLOTS * HEADS)], [PHASES, SLOTS], [0, HEADS]])
                                      ).then_inc(pexp_ready, 1)

            def gate_shift():
                dve.wait_ge(glog_ready, 1)
                bg = wp[:, W_BG:W_BG + ND]
                link(nc.vector.tensor_tensor(glog[:], ps[:, ST, 32:32 + PHASES * ND].rearrange("p (h s) -> p h s", s=ND),
                                             view(wp, W_BG, [[0, PHASES], [1, ND]]), ALU.add))
                link(nc.vector.tensor_reduce(gmax[:], glog[:], AX.X, ALU.max))
                nc.vector.tensor_tensor(gsh[:], glog[:], view(gmax, 0, [[1, PHASES], [0, ND]]),
                                        ALU.subtract).then_inc(gshift_ready, 1)

            def gate_pick():
                dve.wait_ge(gexp_ready, 1)
                link(nc.vector.tensor_reduce(gsum[:], gex[:], AX.X, ALU.add))
                link(nc.vector.reciprocal(grec[:], gsum[:]))
                link(nc.vector.tensor_tensor(gpick[:], gex[:], view(cs, C_DIL, [[0, PHASES], [1, ND]]), ALU.mult))
                link(nc.vector.tensor_reduce(gsel[:], gpick[:], AX.X, ALU.add))
                link(nc.vector.tensor_tensor(gate[:], gsel[:], grec[:], ALU.mult))

            def multiply_qk(ph, s):
                if ph == 0:
                    dve.wait_ge(proj_copied, 2 * s + 2)
                else:
                    dve.wait_ge(scores_ready, s + 1)
                for ci in range(3):
                    c0, c1, co = columns(DIL[s], ci)
                    nc_ = c1 - c0
                    for n, ri, dri, r0, dr, a0, da, rows in pieces(s):
                        o = view(qk[s], (3 * ci + ri) * N + r0 * W + c0, [[dri * N + dr * W, n], [W, rows], [1, nc_]])
                        a = view(q, (s * PHASES + ph) * N + r0 * W + c0, [[dr * W, n], [W, rows], [1, nc_]])
                        b = view(k[s], (ph * ROWS[s] + a0) * W + c0 + co, [[da * W, n], [W, rows], [1, nc_]])
                        last = nc.vector.tensor_tensor(o, a, b, ALU.mult)
                last.then_inc(qk_ready, 1)

            def softmax_shift(ph):
                dve.wait_ge(scores_ready, ND * (ph + 1))
                link(nc.vector.tensor_reduce(smax[:], view(ps, 512 * SC, [[1, QP], [QP, KK]]), AX.X, ALU.max))
                if ph:
                    dve.wait_ge(exp_ready, ph)
                nc.vector.tensor_tensor(shifted[:], view(ps, 512 * SC, [[QP, KK], [1, QP]]),
                                        view(smax, 0, [[0, KK], [1, QP]]), ALU.subtract).then_inc(shift_ready, 1)

            def softmax_divide(ph):
                dve.wait_ge(exp_ready, ph + 1)
                link(nc.vector.tensor_reduce(ssum[:], view(expd, 0, [[1, QP], [QP, KK]]), AX.X, ALU.add))
                link(nc.vector.reciprocal(srec[:], ssum[:]))
                nc.vector.scalar_tensor_tensor(out=prob[:, ph, :, :], in0=expd[:], scalar=gate[:, ph:ph + 1],
                                               in1=view(srec, 0, [[0, KK], [1, QP]]), op0=ALU.mult, op1=ALU.mult
                                               ).then_inc(prob_ready, 1)

            def multiply_pv(ph, s, part):
                ci = CENTRE_FIRST[part]
                c = 12 * ph + 3 * s + part
                if c == 0:
                    dve.wait_ge(proj_copied, len(tiles))
                dve.wait_ge(spread_ready, c + 1)
                if ph and part == 0:
                    dve.wait_ge(added, ADDS * (s + 1))
                c0, c1, co = columns(DIL[s], ci)
                nc_ = c1 - c0
                for n, ri, dri, r0, dr, a0, da, rows in pieces(s):
                    o = view(pv[s], (3 * ci + ri) * N + r0 * W + c0, [[dri * N + dr * W, n], [W, rows], [1, nc_]])
                    if ci == 1 and n == 1:
                        o = view(acc, (ph * ND + s) * N, [[W, rows], [1, nc_]])
                    a = view(ps, 1024 * (c % 2) + 64 * r0 + W * ri + c0, [[W * dri + 64 * dr, n], [64, rows], [1, nc_]])
                    b = view(v[s], (ph * ROWS[s] + a0) * W + c0 + co, [[da * W, n], [W, rows], [1, nc_]])
                    last = nc.vector.tensor_tensor(o, a, b, ALU.mult)
                last.then_inc(pv_ready, 1)

            batches = [range(ph, B, PHASES) for ph in range(PHASES)]

            def first_residual(ph):
                dve.wait_ge(restored, ph + 1)
                for half in range(2):
                    last = nc.vector.tensor_tensor(x1ph[:, ph, 2 * half:2 * half + 2, :],
                                                   xph[:, ph, 2 * half:2 * half + 2, :],
                                                   ps[:, LS + half, :].rearrange("p (j n) -> p j n", j=2), ALU.add)
                link(last)
                channel_stats(x1, batches[ph], ph + 1)

            def copy_pT(ph):
                for half in range(2):
                    dve.wait_ge(pT_ready, SLOTS * ph + 2 * half + 2)
                    nc.vector.tensor_tensor(pT[:, 2 * half:2 * half + 2, :, :].rearrange("p j t n -> p (j t) n"),
                                            ps[:, LP + half, :].rearrange("p (a n) -> p a n", n=P),
                                            view(wp, W_B1R, [[0, 4], [1, P]]), ALU.add).then_inc(pT_copied, 1)

            def attention_shift(ph):
                dve.wait_ge(att_ready, ph + 1)
                att = ps[:, LS, 0:SLOTS * HD1].rearrange("p (j e) -> p j e", e=HD1)
                link(nc.vector.tensor_reduce(amax[:], att, AX.X, ALU.max))
                nc.vector.tensor_tensor(ash[:], att, view(amax, 0, [[1, SLOTS], [0, HD1]]),
                                        ALU.subtract).then_inc(ashift_ready, 1)

            def attention_divide(ph):
                dve.wait_ge(aexp_ready, ph + 1)
                link(nc.vector.tensor_reduce(asum[:], aex[:], AX.X, ALU.add))
                link(nc.vector.reciprocal(arec[:], asum[:]))
                link(nc.vector.tensor_tensor(anorm[:], aex[:], view(arec, 0, [[1, SLOTS], [0, HD1]]), ALU.mult))
                nc.vector.tensor_tensor(ablk[:].rearrange("p j (h e) -> p j h e", h=H1),
                                        view(anorm, 0, [[HD1, SLOTS], [0, H1], [1, HD1]]),
                                        view(cs, C_BLK, [[0, SLOTS], [HD1, H1], [1, HD1]]),
                                        ALU.mult).then_inc(ablk_ready, 1)

            def output_bias(ph):
                dve.wait_ge(mwT_ready, ph + 1)
                nc.vector.tensor_scalar(obias[:], ps[:, LP + 1, 0:SLOTS], wp[:, W_BP:W_BP + 1], None,
                                        ALU.add).then_inc(obias_ready, 1)
                dve.wait_ge(obias_ready, ph + 1)

            def second_residual(ph):
                for j in range(SLOTS):
                    b = PHASES * j + ph
                    dve.wait_ge(fin_ready, SLOTS * ph + (j // 2) * 2 + 2)
                    nc.vector.scalar_tensor_tensor(out=ot[:, b, :], in0=ps[:, LS + j // 2, N * (j % 2):N * (j % 2) + N],
                                                   scalar=obias[:, j:j + 1], in1=x1[:, b, :], op0=ALU.add,
                                                   op1=ALU.add).then_inc(out_ready, 1)

            def second_block(ph):
                bs = slice(ph, B, PHASES)
                return [lambda: first_residual(ph), lambda: group_variance(bs, SLOTS, LP, ph + 1),
                        lambda: norm_bias(bs, ph + 1), lambda: copy_pT(ph), lambda: attention_shift(ph),
                        lambda: attention_divide(ph), lambda: output_bias(ph), lambda: second_residual(ph)]

            for s in range(ND):
                multiply_qk(0, s)
            gate_shift()
            multiply_qk(1, 0)
            gate_pick()
            softmax_shift(0)
            multiply_qk(1, 1)
            softmax_divide(0)
            for s in range(ND):
                for part in range(3):
                    multiply_pv(0, s, part)
                if s + 2 < ND:
                    multiply_qk(1, s + 2)
                if s == 2:
                    softmax_shift(1)
            softmax_divide(1)
            second = second_block(0)
            for c in range(12):
                multiply_pv(1, c // 3, c % 3)
                if c in SECOND_AFTER:
                    second.pop(0)()
            for step in second + second_block(1):
                step()

        @block.tensor
        def _(pe):
            def mm(o, w, m, start=True, stop=True):
                return nc.tensor.matmul(o, w, m, start=start, stop=stop)

            pe.wait_ge(c_loaded, 16)
            pe.wait_ge(stats_ready, 1)
            mm(ps[:, ST, 0:2 * B], cs[:, C_GRP:C_GRP + P], mv[:].rearrange("p b t -> p (b t)")).then_inc(gstats_ready, 1)
            pe.wait_ge(w_loaded, 16)
            pe.wait_ge(xn_ready, B)
            for n, (kind, s) in enumerate(tiles):
                if n >= PROJ_BANKS:
                    pe.wait_ge(proj_copied, n - PROJ_BANKS + 1)
                w0 = W_QKV + P * kind + CD * s
                for j in range(SLOTS):
                    last = mm(ps[32 * j:32 * j + 32, n % PROJ_BANKS, :], wp[:, w0:w0 + CD],
                              xn[:, 2 * j:2 * j + 2, :].rearrange("p h n -> p (h n)"))
                last.then_inc(proj_ready, 1)
                if n == 7:
                    pe.wait_ge(pexp_ready, PHASES)
                    pe.wait_ge(var_ready, 1)
                    for ph in range(PHASES):
                        last = mm(ps[:, ST, 32 + ND * ph:32 + ND * ph + ND], pexp[:, ph, :], wp[:, W_GATE:W_GATE + ND])
                    last.then_inc(glog_ready, 1)

            def sum_scores(ph, s):
                if s == 0:
                    if ph:
                        pe.wait_ge(shift_ready, ph)
                    else:
                        pe.wait_ge(proj_copied, len(tiles))
                pe.wait_ge(qk_ready, ND * ph + s + 1)
                w = cs[:, C_RED + 32 * s:C_RED + 32 * s + 32]
                for a, b, bank in ((0, 8, SC), (8, 9, SC + 1)):
                    for j in range(4):
                        last = mm(ps[32 * j:32 * j + 32, bank, 0:(b - a) * QP].rearrange("p (o n) -> p o n", n=QP), w,
                                  qk[s][:, a:b, QP * j:QP * j + QP], start=(s == 0), stop=(s == ND - 1))
                last.then_inc(scores_ready, 1)

            def spread(ph, s):
                if s == 0:
                    pe.wait_ge(prob_ready, ph + 1)
                for part, ci in enumerate(CENTRE_FIRST):
                    c = 12 * ph + 3 * s + part
                    if c >= 2:
                        pe.wait_ge(pv_ready, c - 1)
                    c0, c1, _ = columns(DIL[s], ci)
                    for j in range(4):
                        i0, i1 = row_offsets(s, j)
                        dims = lambda slot, row: [[slot, i1 - i0], [row, QR], [1, c1 - c0]]
                        o = view(ps, 1024 * (c % 2) + 64 * QR * j + W * i0 + c0, dims(W, 64))
                        m = view(prob, (ph * KK + 3 * ci + i0) * QP + c0, dims(QP, W))
                        last = mm(o, sel[:, j, s, :], m)
                    last.then_inc(spread_ready, 1)

            def restore(ph):
                pe.wait_ge(added, ADDS * ND * (ph + 1))
                if ph:
                    pe.wait_ge(out_ready, SLOTS * ph)
                for j in range(SLOTS):
                    for s in range(ND):
                        last = mm(ps[32 * s:32 * s + 32, LS + j // 2, N * (j % 2):N * (j % 2) + N],
                                  ident[:, 32 * j:32 * j + 32], acc[:, ph, s, :])
                last.then_inc(restored, 1)

            def group_stats(ph):
                pe.wait_ge(stats_ready, ph + 2)
                if ph:
                    pe.wait_ge(mwT_copied, ph)
                else:
                    pe.wait_ge(shift_ready, PHASES)
                mm(ps[:, LP, 0:2 * SLOTS].rearrange("p (j t) -> p j t", t=2), cs[:, C_GRP:C_GRP + P],
                   mvph[:, ph, :, :]).then_inc(gstats_ready, 1)

            def project_tokens(ph):
                pe.wait_ge(var_ready, ph + 2)
                if ph:
                    pe.wait_ge(obias_ready, ph)
                for j in range(SLOTS):
                    pe.wait_ge(xn1_ready, SLOTS * ph + j + 1)
                    for t in range(2):
                        last = mm(ps[:, LP + j // 2, 256 * (j % 2) + P * t:256 * (j % 2) + P * t + P],
                                  xn1[:, j, P * t:P * t + P], wp[:, W_1T:W_1T + P])
                    last.then_inc(pT_ready, 1)

            def attention(ph):
                for j in range(SLOTS):
                    if j % 2 == 0:
                        pe.wait_ge(pT_copied, 2 * ph + j // 2 + 1)
                    for t in range(2):
                        for h in range(H1):
                            last = mm(ps[32 * h:32 * h + 32, LS, HD1 * j:HD1 * j + HD1], pT[:, j, t, HD1 * h:HD1 * h + HD1],
                                      pT[:, j, t, HD1 * h:HD1 * h + HD1], start=(t == 0), stop=(t == 1))
                last.then_inc(att_ready, 1)

            def fuse(ph):
                pe.wait_ge(ablk_ready, ph + 1)
                for j in range(SLOTS):
                    last = mm(ps[:, LS + 1, P * j:P * j + P], ablk[:, j, :], wp[:, W_PT:W_PT + P])
                last.then_inc(mT_ready, 1)

            def fuse_projection(ph):
                pe.wait_ge(mT_copied, ph + 1)
                for j in range(SLOTS):
                    mm(ps[:, LP, P * j:P * j + P], wp[:, W_1:W_1 + P], mT[:, j, :])
                for j in range(SLOTS):
                    last = mm(ps[:, LP + 1, j:j + 1], mT[:, j, :], wp[:, W_B1:W_B1 + 1])
                last.then_inc(mwT_ready, 1)

            def finish(ph):
                pe.wait_ge(mwT_copied, ph + 1)
                for j in range(SLOTS):
                    mm(ps[:, LS + j // 2, N * (j % 2):N * (j % 2) + N], mwT[:, j, :], xn1[:, j, :]).then_inc(fin_ready, 1)

            second = [restore, group_stats, project_tokens, attention, fuse, fuse_projection, finish]
            for s in range(ND):
                sum_scores(0, s)
            pe.wait_ge(sel_loaded, 64)
            sum_scores(1, 0)
            sum_scores(1, 1)
            spread(0, 0)
            spread(0, 1)
            sum_scores(1, 2)
            spread(0, 2)
            sum_scores(1, 3)
            spread(0, 3)
            for s in range(ND):
                spread(1, s)
                for step in SECOND_PE[s]:
                    second[step](0)
            for step in second:
                step(1)


def kernel(**inputs):
    import numpy as np
    import concourse.bacc as bacc
    from concourse.bass_utils import run_bass_kernel_spmd

    def get(name):
        return np.asarray(inputs[name])

    w1, b1 = get("L1_conv_W_qkv"), get("L1_conv_b_qkv")
    wpack = np.concatenate([
        get("L0_conv_w_qkv").T, get("L0_conv_w_gate").T, w1, w1.T, get("L1_conv_W_proj").T, b1[:, None],
        get("L1_conv_b_proj")[:, None], np.broadcast_to(b1, (P, P)), np.broadcast_to(get("L0_conv_b_gate"), (P, ND))],
        axis=1)
    p = np.arange(P)
    score = np.arange(32)
    head_of = 2 * (p // CD) + p % CD // HD
    reduce_ = np.zeros((P, ND, 32), np.float32)
    for s in range(ND):
        reduce_[p, s, 8 * s + head_of] = 1
    consts = np.concatenate([
        np.eye(P, dtype=np.float32), (p[:, None] // GC == p // GC).astype(np.float32) / GC, reduce_.reshape(P, -1),
        (p[:, None] // HD1 == p // HD1).astype(np.float32),
        (p[:, None] % 32 // 8 == np.arange(ND)).astype(np.float32)], axis=1)
    selc = np.zeros((32, ND, P), np.float32)
    for s in range(ND):
        selc[:, s, :] = score[:, None] == 8 * s + head_of
    arrays = {"x_dram": np.ascontiguousarray(get("x").reshape(B, P, N)),
              "wpack_dram": np.ascontiguousarray(wpack), "consts_dram": np.ascontiguousarray(consts),
              "selc_dram": selc}
    nc = bacc.Bacc("TRN2", target_bir_lowering=False, num_devices=1)
    args = [nc.dram_tensor(n, a.shape, mybir.dt.from_np(a.dtype), kind="ExternalInput").ap() for n, a in arrays.items()]
    out = nc.dram_tensor("out_dram", (B, P, N), F32, kind="ExternalOutput").ap()
    build(nc, *args, out)
    r = run_bass_kernel_spmd(nc, [arrays], core_ids=[0])
    return r.results[0]["out_dram"].reshape(B, P, H, W)
```

```python
from contextlib import ExitStack

import concourse.bass as bass
from concourse import mybir

P = 128
B, H, W = 8, 16, 16
N = H * W
DIL = (1, 2, 4, 8)
ND = len(DIL)
CD = P // ND
HEADS = 2
HD = CD // HEADS
KK = 9
PHASES = 2
SLOTS = B // PHASES
QP = N // 4
QR = H // 4
GC = 4
H1 = 4
HD1 = P // H1
PAD = [d if d < 4 else 0 for d in DIL]
ROWS = [H + 2 * p for p in PAD]
EPS = 1e-5
SCALE0 = float(HD) ** -0.5
SCALE1 = float(N) ** -0.5
CENTRE_FIRST = (1, 0, 2)
GB = 2
GROUPS = B // GB
NORM_ON_ACT = (1, 3, 5)


DVE_BETWEEN = {8: ((0, 0),), 9: ((0, 1),), 10: ((1, 0),), 11: ((1, 1), (2, 0))}
PE_BETWEEN = {2: ((0, 0), (0, 1)), 3: ((1, 0), (1, 1))}
RSQRT_AFTER = ((1, 4), (1, 7))
PE_CHAIN, DVE_CHAIN, ACT_CHAIN = (0, 2, 7, 9, 13, 15, 17), (1, 3, 5, 8, 10, 12, 18), (6, 11, 14, 16)
START = (0, 2, 5, 8)


def order(chain, between=()):
    every = [(step, g) for step in range(len(chain)) for g in range(GROUPS)]
    taken = [x for xs in dict(between).values() for x in xs]
    return sorted((x for x in every if x not in taken), key=lambda x: (chain[x[0]] + START[x[1]], x[1]))



F32 = mybir.dt.float32
ALU = mybir.AluOpType
ACT = mybir.ActivationFunctionType
AX = mybir.AxisListType

W_QKV, W_GATE, W_1, W_1T, W_PT, W_B1, W_BP, W_B1R, W_BG, W_END = 0, 384, 388, 516, 644, 772, 773, 774, 902, 906
C_ID, C_GRP, C_RED, C_BLK, C_DIL, C_END = 0, 128, 256, 384, 512, 516


def columns(d, ci):
    co = (ci - 1) * d
    return max(0, -co), min(W, W - co), co


def pieces(s):
    d = DIL[s]
    if PAD[s]:
        return [(3, 0, 1, 0, 0, 0, d, H)]
    return [(1, 1, 0, 0, 0, 0, 0, H), (2, 0, 2, d, -d, 0, d, H - d)]


def row_offsets(s, j):
    if PAD[s]:
        return 0, 3
    return (0 if QR * j >= DIL[s] else 1), (3 if QR * j + DIL[s] < H else 2)


def additions(s):
    pairs = [(3 * ci + 1, 3 * ci + ri) for ci, ri in ((1, 0), (0, 0), (1, 2), (0, 2), (2, 0))]
    pairs += [(4, 1), (7, 8), (4, 7)]
    after = [None, None, 0, 1, None, 3, 4, 6]
    return [(t, a, f) for (t, a), f in zip(pairs, after)]


ADDS = len(additions(0))
ADD_NEEDS = (1, 2, 2, 2, 3, 3, 3, 3)
POOL_SUMS = (ND, 2)


def valid_rows(s, ri):
    if PAD[s]:
        return 0, H
    ro = (ri - 1) * DIL[s]
    return max(0, -ro), min(H, H - ro)


def view(t, offset, dims):
    return bass.AP(t, offset, [[t[:].ap[0][0], P]] + [list(x) for x in dims if x[1] > 1])


def build(nc, x, wpack, consts, selc, out):
    with ExitStack() as ctx:
        def sb(name, shape):
            return ctx.enter_context(nc.sbuf_tensor(name, shape, F32))

        def sem(name):
            return ctx.enter_context(nc.semaphore(name))

        xt = sb("xt", [P, B, N])
        xn = sb("xn", [P, B, N])
        wp = sb("wp", [P, W_END])
        cs = sb("cs", [P, C_END])
        sel = sb("sel", [P, 4, ND, P])
        q = sb("q", [P, ND, PHASES, N])
        k = [sb(f"k{s}", [P, PHASES, ROWS[s], W]) for s in range(ND)]
        v = [sb(f"v{s}", [P, PHASES, ROWS[s], W]) for s in range(ND)]
        qk = [sb(f"qk{s}", [P, KK, N]) for s in range(ND)]
        pv = [sb(f"pv{s}", [P, KK, N]) for s in range(ND)]
        acc = sb("acc", [P, PHASES, ND, N])
        shifted = sb("shifted", [P, KK, QP])
        expd = sb("expd", [P, KK, QP])
        prob = sb("prob", [P, PHASES, KK, QP])
        smax = sb("smax", [P, QP])
        ssum = sb("ssum", [P, QP])
        srec = sb("srec", [P, QP])
        bst = sb("bst", [P, B, 6])
        mv = sb("mv", [P, B, 2])
        msq = sb("msq", [P, B])
        gst = sb("gst", [P, B, 2])
        gsq = sb("gsq", [P, B])
        gvar = sb("gvar", [P, B])
        mhalf = sb("mhalf", [P, B])
        rstd = sb("rstd", [P, B])
        nbias = sb("nbias", [P, B])
        warm = sb("warm", [P, 1])
        pooled = sb("pooled", [P, B])
        pexp = sb("pexp", [P, PHASES, P])
        glog = sb("glog", [P, PHASES, ND])
        gsh = sb("gsh", [P, PHASES, ND])
        gex = sb("gex", [P, PHASES, ND])
        gpick = sb("gpick", [P, PHASES, ND])
        gmax = sb("gmax", [P, PHASES])
        gsum = sb("gsum", [P, PHASES])
        grec = sb("grec", [P, PHASES])
        gsel = sb("gsel", [P, PHASES])
        gate = sb("gate", [P, PHASES])
        x1 = sb("x1", [P, B, N])
        xn1 = sb("xn1", [P, GROUPS, GB, N])
        pT = sb("pT", [P, GROUPS, GB * 2, P])
        amax = sb("amax", [P, GROUPS, GB])
        ash = sb("ash", [P, GROUPS, GB, HD1])
        aex = sb("aex", [P, GROUPS, GB, HD1])
        asum = sb("asum", [P, GROUPS, GB])
        arec = sb("arec", [P, GROUPS, GB])
        anorm = sb("anorm", [P, GROUPS, GB, HD1])
        ablk = sb("ablk", [P, GROUPS, GB, P])
        mT = sb("mT", [P, GROUPS, GB, P])
        mwT = sb("mwT", [P, GROUPS, GB, P])
        obias = sb("obias", [P, GROUPS, GB])

        ps = ctx.enter_context(nc.psum_tensor("ps", [P, 8, 512], F32))
        SC = 4
        ST = 7
        PROJ_BANKS = (0, 1, 2, 3, 6)
        FIRST_BANK, SECOND_BANK = (4, 6, 0, 2), (5, 7, 1, 3)

        x_loaded = [sem(f"x_loaded{i}") for i in range(4)]
        w_loaded = sem("w_loaded")
        c_loaded = sem("c_loaded")
        sel_zeroed = sem("sel_zeroed")
        sel_loaded = sem("sel_loaded")
        halo_zeroed = sem("halo_zeroed")
        dve_settled = sem("dve_settled")
        mhalf_set = sem("mhalf_set")
        stats_ready = sem("stats_ready")
        gstats_ready = sem("gstats_ready")
        nbias_ready = sem("nbias_ready")
        var_ready = sem("var_ready")
        rstd_ready = sem("rstd_ready")
        xn_ready = sem("xn_ready")
        xn_act_ready = sem("xn_act_ready")
        pexp_ready = sem("pexp_ready")
        glog_ready = sem("glog_ready")
        gshift_ready = sem("gshift_ready")
        gexp_ready = sem("gexp_ready")
        proj_ready = sem("proj_ready")
        proj_copied = sem("proj_copied")
        qk_ready = sem("qk_ready")
        scores_ready = sem("scores_ready")
        shift_ready = sem("shift_ready")
        exp_ready = sem("exp_ready")
        prob_ready = sem("prob_ready")
        spread_ready = sem("spread_ready")
        pv_ready = sem("pv_ready")
        added = sem("added")
        dve_added = sem("dve_added")
        restored = sem("restored")
        obias_ready = sem("obias_ready")
        xn1_ready = sem("xn1_ready")
        pT_ready = sem("pT_ready")
        pT_copied = sem("pT_copied")
        att_ready = sem("att_ready")
        ashift_ready = sem("ashift_ready")
        aexp_ready = sem("aexp_ready")
        ablk_ready = sem("ablk_ready")
        mT_ready = sem("mT_ready")
        mT_copied = sem("mT_copied")
        mwT_ready = sem("mwT_ready")
        mwT_copied = sem("mwT_copied")
        fin_ready = sem("fin_ready")
        out_ready = sem("out_ready")
        out_stored = sem("out_stored")

        ident = cs[:, C_ID:C_ID + P]

        def group(g):
            first = PHASES * GB * (g % 2) + g // 2
            return slice(first, first + PHASES * (GB - 1) + 1, PHASES)

        def batch(g, i):
            return group(g).start + PHASES * i

        tiles = [(kind, s) for s in range(ND) for kind in (0, 1)] + [(2, s) for s in range(ND)]
        def operands(ph, s, n, target, slot):
            ci, ri = divmod(slot, 3)
            c0, c1, _ = columns(DIL[s], ci)
            r0, r1 = valid_rows(s, ri)

            def rect(t):
                return t.rearrange("p (r c) -> p r c", c=W)[:, r0:r1, c0:c1]

            o = rect(acc[:, ph, s, :] if target == 4 else pv[s][:, target, :])
            a = rect(pv[s][:, 4, :]) if n == 0 and PAD[s] else o
            return o, a, rect(pv[s][:, slot, :])

        block = ctx.enter_context(nc.Block())

        @block.sync
        def _(sp):
            xv = x.rearrange("b c n -> c b n")
            for i in range(4):
                sp.dma_start(xt[:, 2 * i:2 * i + 2, :], xv[:, 2 * i:2 * i + 2, :]).then_inc(x_loaded[i], 16)
            sp.wait_ge(sel_zeroed, 1)
            for j in range(4):
                sp.dma_start(sel[32 * j:32 * j + 32, j, :, :], selc).then_inc(sel_loaded, 16)
            for n in range(B):
                b = batch(n // GB, n % GB)
                sp.wait_ge(out_ready, n + 1)
                sp.dma_start(out[b], x1[:, b, :]).then_inc(out_stored, 16)
            sp.wait_ge(out_stored, 16 * B)

        @block.gpsimd
        def _(pool):
            nc.gpsimd.memset(mhalf[:], -0.5).then_inc(mhalf_set, 1)
            nc.gpsimd.memset(sel[:], 0.0).then_inc(sel_zeroed, 1)
            for s in range(ND):
                if PAD[s]:
                    for t in (k[s], v[s]):
                        for r in (0, PAD[s] + H):
                            last = nc.gpsimd.memset(t[:, :, r:r + PAD[s], :], 0.0)
            last.then_inc(halo_zeroed, 1)
            pool.wait_ge(var_ready, 1)
            pool.wait_ge(mhalf_set, 1)
            nc.gpsimd.tensor_tensor(rstd[:], gvar[:], mhalf[:], ALU.pow).then_inc(rstd_ready, 1)

            def rsqrt(g):
                pool.wait_ge(var_ready, g + 2)
                nc.gpsimd.tensor_tensor(rstd[:, group(g)], gvar[:, group(g)], mhalf[:, group(g)],
                                        ALU.pow).then_inc(rstd_ready, 1)

            base = 0
            for ph in range(PHASES):
                for s in range(POOL_SUMS[ph]):
                    for n, (target, slot, after) in enumerate(additions(s)):
                        chunk = 12 * ph + 3 * s + ADD_NEEDS[n]
                        if n == 0 or ADD_NEEDS[n] > ADD_NEEDS[n - 1]:
                            pool.wait_ge(pv_ready, chunk)
                        if after is not None:
                            pool.wait_ge(added, base + after + 1)
                        o, a, b = operands(ph, s, n, target, slot)
                        nc.gpsimd.tensor_tensor(o, a, b, ALU.add).then_inc(added, 1)
                        if ph == 1 and (s, n) in RSQRT_AFTER:
                            rsqrt(RSQRT_AFTER.index((s, n)))
                    base += ADDS
            for g in range(len(RSQRT_AFTER), GROUPS):
                rsqrt(g)

        @block.scalar
        def _(act):
            act.dma_start(wp[:], wpack).then_inc(w_loaded, 16)
            act.dma_start(cs[:], consts).then_inc(c_loaded, 16)
            act.wait_ge(mhalf_set, 1)
            nc.scalar.activation(warm[:], mhalf[:, 0:1], ACT.Exp)
            act.wait_ge(nbias_ready, 1)
            for b in NORM_ON_ACT:
                nc.scalar.activation(xn[:, b, :], xt[:, b, :], ACT.Identity, bias=nbias[:, b:b + 1],
                                     scale=rstd[:, b:b + 1]).then_inc(xn_act_ready, 1)
            act.wait_ge(halo_zeroed, 1)
            for n, (kind, s) in enumerate(tiles):
                act.wait_ge(proj_ready, n + 1)
                src = ps[:, PROJ_BANKS[n % len(PROJ_BANKS)], :]
                if kind == 0:
                    nc.scalar.copy(q[:, s, :, :], src.rearrange("p (h n) -> p h n", h=PHASES)).then_inc(proj_copied, 1)
                else:
                    dst = (k, v)[kind - 1][s][:, :, PAD[s]:PAD[s] + H, :]
                    nc.scalar.copy(dst, src.rearrange("p (h r c) -> p h r c", h=PHASES, c=W)).then_inc(proj_copied, 1)
            act.wait_ge(gshift_ready, 1)
            nc.scalar.activation(gex[:], gsh[:], ACT.Exp).then_inc(gexp_ready, 1)
            for ph in range(PHASES):
                act.wait_ge(shift_ready, ph + 1)
                if ph:
                    act.wait_ge(prob_ready, ph)
                nc.scalar.activation(expd[:], shifted[:], ACT.Exp, scale=SCALE0).then_inc(exp_ready, 1)

            def norm(g):
                act.wait_ge(nbias_ready, g + 2)
                for i in range(GB):
                    b = batch(g, i)
                    nc.scalar.activation(xn1[:, g, i, :], x1[:, b, :], ACT.Identity, bias=nbias[:, b:b + 1],
                                         scale=rstd[:, b:b + 1]).then_inc(xn1_ready, 1)

            def attention_exp(g):
                act.wait_ge(ashift_ready, g + 1)
                nc.scalar.activation(aex[:, g], ash[:, g], ACT.Exp, scale=SCALE1).then_inc(aexp_ready, 1)

            def copy_fused(g):
                act.wait_ge(mT_ready, g + 1)
                nc.scalar.copy(mT[:, g], ps[:, FIRST_BANK[g], 0:GB * P].rearrange("p (i n) -> p i n", i=GB)
                               ).then_inc(mT_copied, 1)

            def copy_fused_projection(g):
                act.wait_ge(mwT_ready, g + 1)
                nc.scalar.copy(mwT[:, g], ps[:, SECOND_BANK[g], 0:GB * P].rearrange("p (i n) -> p i n", i=GB)
                               ).then_inc(mwT_copied, 1)

            steps = (norm, attention_exp, copy_fused, copy_fused_projection)
            for step, g in order(ACT_CHAIN):
                steps[step](g)

        @block.vector
        def _(dve):
            settled = [0]

            def link(ins):
                settled[0] += 1
                ins.then_inc(dve_settled, 1)
                dve.wait_ge(dve_settled, settled[0])

            for s, d in enumerate(DIL):
                t = qk[s][:].rearrange("p (a i) (r c) -> p a (i r) c", i=3, c=W)
                nc.vector.memset(t[:, 0, :, 0:d], 0.0)
                last = nc.vector.memset(t[:, 2, :, W - d:W], 0.0)
            link(last)
            for s, d in enumerate(DIL):
                if not PAD[s]:
                    t = qk[s][:].rearrange("p (a i) n -> p a i n", i=3)
                    nc.vector.memset(t[:, :, 0, 0:d * W], 0.0)
                    last = nc.vector.memset(t[:, :, 2, (H - d) * W:N], 0.0)
            link(last)

            def channel_stats(src, bs):
                for b in range(B)[bs]:
                    if src is xt and b % 2 == 0:
                        dve.wait_ge(x_loaded[b // 2], 16)
                    last = nc.vector.bn_stats(bst[:, b, :], src[:, b, :])
                link(last)
                for b in range(B)[bs]:
                    last = nc.vector.bn_aggr(mv[:, b, :], bst[:, b, :])
                link(last)
                link(nc.vector.tensor_tensor(msq[:, bs], mv[:, bs, 0], mv[:, bs, 0], ALU.mult))
                nc.vector.tensor_tensor(mv[:, bs, 1], mv[:, bs, 1], msq[:, bs], ALU.add).then_inc(stats_ready, 1)

            def group_variance(bs, n, bank, g):
                dve.wait_ge(gstats_ready, g + 1)
                link(nc.vector.tensor_copy(gst[:, bs, :], ps[:, bank, 0:2 * n].rearrange("p (b t) -> p b t", t=2)))
                link(nc.vector.tensor_tensor(gsq[:, bs], gst[:, bs, 0], gst[:, bs, 0], ALU.mult))
                nc.vector.scalar_tensor_tensor(out=gvar[:, bs], in0=gst[:, bs, 1], scalar=EPS, in1=gsq[:, bs],
                                               op0=ALU.add, op1=ALU.subtract).then_inc(var_ready, 1)

            def norm_bias(bs, g):
                dve.wait_ge(rstd_ready, g + 1)
                nc.vector.scalar_tensor_tensor(out=nbias[:, bs], in0=gst[:, bs, 0], scalar=-1.0, in1=rstd[:, bs],
                                               op0=ALU.mult, op1=ALU.mult).then_inc(nbias_ready, 1)

            every = slice(0, B)
            channel_stats(xt, every)
            group_variance(every, B, ST, 0)
            norm_bias(every, 0)
            dve.wait_ge(nbias_ready, 1)
            for b in range(B):
                if b not in NORM_ON_ACT:
                    nc.vector.tensor_scalar(xn[:, b, :], xt[:, b, :], rstd[:, b:b + 1], nbias[:, b:b + 1],
                                            ALU.mult, ALU.add).then_inc(xn_ready, 1)
            link(nc.vector.tensor_tensor(pooled[:], mv[:, :, 0], rstd[:], ALU.mult))
            link(nc.vector.tensor_tensor(pooled[:], pooled[:], nbias[:], ALU.add))
            for ph in range(PHASES):
                dst = pexp[:, ph, :].rearrange("p (i j h) -> p i j h", j=SLOTS, h=HEADS)
                nc.vector.tensor_copy(dst, view(pooled, ph, [[0, P // (SLOTS * HEADS)], [PHASES, SLOTS], [0, HEADS]])
                                      ).then_inc(pexp_ready, 1)

            def gate_shift():
                dve.wait_ge(glog_ready, 1)
                bg = wp[:, W_BG:W_BG + ND]
                link(nc.vector.tensor_tensor(glog[:], ps[:, ST, 32:32 + PHASES * ND].rearrange("p (h s) -> p h s", s=ND),
                                             view(wp, W_BG, [[0, PHASES], [1, ND]]), ALU.add))
                link(nc.vector.tensor_reduce(gmax[:], glog[:], AX.X, ALU.max))
                nc.vector.tensor_tensor(gsh[:], glog[:], view(gmax, 0, [[1, PHASES], [0, ND]]),
                                        ALU.subtract).then_inc(gshift_ready, 1)

            def gate_pick():
                dve.wait_ge(gexp_ready, 1)
                link(nc.vector.tensor_reduce(gsum[:], gex[:], AX.X, ALU.add))
                link(nc.vector.reciprocal(grec[:], gsum[:]))
                link(nc.vector.tensor_tensor(gpick[:], gex[:], view(cs, C_DIL, [[0, PHASES], [1, ND]]), ALU.mult))
                link(nc.vector.tensor_reduce(gsel[:], gpick[:], AX.X, ALU.add))
                link(nc.vector.tensor_tensor(gate[:], gsel[:], grec[:], ALU.mult))

            def multiply_qk(ph, s, ci):
                if ph == 0:
                    dve.wait_ge(proj_copied, 2 * s + 2)
                elif ci == 0:
                    dve.wait_ge(scores_ready, s + 1)
                c0, c1, co = columns(DIL[s], ci)
                for n, ri, dri, r0, dr, a0, da, rows in pieces(s):
                    o = view(qk[s], (3 * ci + ri) * N + r0 * W + c0, [[dri * N + dr * W, n], [W, rows], [1, c1 - c0]])
                    a = view(q, (s * PHASES + ph) * N + r0 * W + c0, [[dr * W, n], [W, rows], [1, c1 - c0]])
                    b = view(k[s], (ph * ROWS[s] + a0) * W + c0 + co, [[da * W, n], [W, rows], [1, c1 - c0]])
                    last = nc.vector.tensor_tensor(o, a, b, ALU.mult)
                if ci == 2:
                    last.then_inc(qk_ready, 1)

            def softmax_shift(ph):
                dve.wait_ge(scores_ready, ND * (ph + 1))
                link(nc.vector.tensor_reduce(smax[:], view(ps, 512 * SC, [[1, QP], [QP, KK]]), AX.X, ALU.max))
                if ph:
                    dve.wait_ge(exp_ready, ph)
                nc.vector.tensor_tensor(shifted[:], view(ps, 512 * SC, [[QP, KK], [1, QP]]),
                                        view(smax, 0, [[0, KK], [1, QP]]), ALU.subtract).then_inc(shift_ready, 1)

            def softmax_divide(ph):
                dve.wait_ge(exp_ready, ph + 1)
                link(nc.vector.tensor_reduce(ssum[:], view(expd, 0, [[1, QP], [QP, KK]]), AX.X, ALU.add))
                link(nc.vector.reciprocal(srec[:], ssum[:]))
                nc.vector.scalar_tensor_tensor(out=prob[:, ph, :, :], in0=expd[:], scalar=gate[:, ph:ph + 1],
                                               in1=view(srec, 0, [[0, KK], [1, QP]]), op0=ALU.mult, op1=ALU.mult
                                               ).then_inc(prob_ready, 1)

            def multiply_pv(ph, s, part):
                ci = CENTRE_FIRST[part]
                c = 12 * ph + 3 * s + part
                if c == 0:
                    dve.wait_ge(proj_copied, len(tiles))
                dve.wait_ge(spread_ready, c + 1)
                if ph and part == 0:
                    dve.wait_ge(added, ADDS * (s + 1))
                c0, c1, co = columns(DIL[s], ci)
                nc_ = c1 - c0
                for n, ri, dri, r0, dr, a0, da, rows in pieces(s):
                    o = view(pv[s], (3 * ci + ri) * N + r0 * W + c0, [[dri * N + dr * W, n], [W, rows], [1, nc_]])
                    if ci == 1 and n == 1:
                        o = view(acc, (ph * ND + s) * N, [[W, rows], [1, nc_]])
                    a = view(ps, 1024 * (c % 2) + 64 * r0 + W * ri + c0, [[W * dri + 64 * dr, n], [64, rows], [1, nc_]])
                    b = view(v[s], (ph * ROWS[s] + a0) * W + c0 + co, [[da * W, n], [W, rows], [1, nc_]])
                    last = nc.vector.tensor_tensor(o, a, b, ALU.mult)
                last.then_inc(pv_ready, 1)

            def add_neighbours(ph, s):
                done = ADDS * (s - POOL_SUMS[ph])
                for n, (target, slot, after) in enumerate(additions(s)):
                    if n == 0 or ADD_NEEDS[n] > ADD_NEEDS[n - 1]:
                        dve.wait_ge(pv_ready, 12 * ph + 3 * s + ADD_NEEDS[n])
                    if after is not None:
                        dve.wait_ge(dve_added, done + after + 1)
                    o, a, b = operands(ph, s, n, target, slot)
                    nc.vector.tensor_tensor(o, a, b, ALU.add).then_inc(dve_added, 1)

            def first_residual(g):
                dve.wait_ge(restored, g + 1)
                link(nc.vector.tensor_tensor(x1[:, group(g), :], xt[:, group(g), :],
                                             ps[:, FIRST_BANK[g], :].rearrange("p (i n) -> p i n", i=GB), ALU.add))
                channel_stats(x1, group(g))

            def second_variance(g):
                group_variance(group(g), GB, SECOND_BANK[g], g + 1)

            def second_norm_bias(g):
                norm_bias(group(g), g + 1)

            def copy_pT(g):
                dve.wait_ge(pT_ready, g + 1)
                nc.vector.tensor_tensor(pT[:, g], ps[:, FIRST_BANK[g], :].rearrange("p (a n) -> p a n", n=P),
                                        view(wp, W_B1R, [[0, 2 * GB], [1, P]]), ALU.add).then_inc(pT_copied, 1)

            def attention_shift(g):
                dve.wait_ge(att_ready, g + 1)
                att = ps[:, SECOND_BANK[g], 0:GB * HD1].rearrange("p (i e) -> p i e", e=HD1)
                link(nc.vector.tensor_reduce(amax[:, g], att, AX.X, ALU.max))
                nc.vector.tensor_tensor(ash[:, g], att, view(amax, GB * g, [[1, GB], [0, HD1]]),
                                        ALU.subtract).then_inc(ashift_ready, 1)

            def attention_divide(g):
                dve.wait_ge(aexp_ready, g + 1)
                link(nc.vector.tensor_reduce(asum[:, g], aex[:, g], AX.X, ALU.add))
                link(nc.vector.reciprocal(arec[:, g], asum[:, g]))
                link(nc.vector.tensor_tensor(anorm[:, g], aex[:, g], view(arec, GB * g, [[1, GB], [0, HD1]]), ALU.mult))
                nc.vector.tensor_tensor(ablk[:, g].rearrange("p i (h e) -> p i h e", h=H1),
                                        view(anorm, GB * HD1 * g, [[HD1, GB], [0, H1], [1, HD1]]),
                                        view(cs, C_BLK, [[0, GB], [HD1, H1], [1, HD1]]),
                                        ALU.mult).then_inc(ablk_ready, 1)

            def second_residual(g):
                dve.wait_ge(mwT_ready, g + 1)
                link(nc.vector.tensor_scalar(obias[:, g], ps[:, FIRST_BANK[g], GB * P:GB * P + GB],
                                             wp[:, W_BP:W_BP + 1], None, ALU.add))
                dve.wait_ge(fin_ready, g + 1)
                for i in range(GB):
                    b = batch(g, i)
                    nc.vector.scalar_tensor_tensor(out=x1[:, b, :], in0=ps[:, SECOND_BANK[g], N * i:N * i + N],
                                                   scalar=obias[:, g, i:i + 1], in1=x1[:, b, :], op0=ALU.add,
                                                   op1=ALU.add).then_inc(out_ready, 1)

            steps = (first_residual, second_variance, second_norm_bias, copy_pT, attention_shift, attention_divide,
                     second_residual)
            for s in range(ND):
                for ci in range(3):
                    multiply_qk(0, s, ci)
            gate_shift()
            for ci in range(3):
                multiply_qk(1, 0, ci)
            gate_pick()
            softmax_shift(0)
            multiply_qk(1, 1, 0)
            softmax_divide(0)
            multiply_qk(1, 1, 1)
            multiply_qk(1, 1, 2)
            for c in range(12):
                multiply_pv(0, c // 3, c % 3)
                if c < 6:
                    multiply_qk(1, 2 + c // 3, c % 3)
                if c == 7:
                    softmax_shift(1)
                if c == 9:
                    softmax_divide(1)
            for c in range(12):
                multiply_pv(1, c // 3, c % 3)
                if c % 3 == 2 and c // 3 >= POOL_SUMS[1]:
                    add_neighbours(1, c // 3)
                for step, g in DVE_BETWEEN.get(c, ()):
                    steps[step](g)
            for step, g in order(DVE_CHAIN, DVE_BETWEEN):
                steps[step](g)

        @block.tensor
        def _(pe):
            def mm(o, w, m, start=True, stop=True):
                return nc.tensor.matmul(o, w, m, start=start, stop=stop)

            pe.wait_ge(c_loaded, 16)
            pe.wait_ge(stats_ready, 1)
            mm(ps[:, ST, 0:2 * B], cs[:, C_GRP:C_GRP + P], mv[:].rearrange("p b t -> p (b t)")).then_inc(gstats_ready, 1)
            def project(n):
                kind, s = tiles[n]
                bank = PROJ_BANKS[n % len(PROJ_BANKS)]
                if n >= len(PROJ_BANKS):
                    pe.wait_ge(proj_copied, n - len(PROJ_BANKS) + 1)
                w0 = W_QKV + P * kind + CD * s
                for j in range(SLOTS):
                    if n == 0:
                        done = [b for b in range(2 * j + 2) if b in NORM_ON_ACT]
                        if done:
                            pe.wait_ge(xn_act_ready, len(done))
                        pe.wait_ge(xn_ready, 2 * j + 2 - len(done))
                    last = mm(ps[32 * j:32 * j + 32, bank, :], wp[:, w0:w0 + CD],
                              xn[:, 2 * j:2 * j + 2, :].rearrange("p h n -> p (h n)"))
                last.then_inc(proj_ready, 1)

            def gate_logits():
                pe.wait_ge(pexp_ready, PHASES)
                pe.wait_ge(var_ready, 1)
                for ph in range(PHASES):
                    last = mm(ps[:, ST, 32 + ND * ph:32 + ND * ph + ND], pexp[:, ph, :], wp[:, W_GATE:W_GATE + ND])
                last.then_inc(glog_ready, 1)

            def sum_scores(ph, s):
                if s == 0 and ph:
                    pe.wait_ge(shift_ready, ph)
                pe.wait_ge(qk_ready, ND * ph + s + 1)
                w = cs[:, C_RED + 32 * s:C_RED + 32 * s + 32]
                for a, b, bank in ((0, 8, SC), (8, 9, SC + 1)):
                    for j in range(4):
                        last = mm(ps[32 * j:32 * j + 32, bank, 0:(b - a) * QP].rearrange("p (o n) -> p o n", n=QP), w,
                                  qk[s][:, a:b, QP * j:QP * j + QP], start=(s == 0), stop=(s == ND - 1))
                last.then_inc(scores_ready, 1)

            def spread(ph, s):
                if s == 0:
                    pe.wait_ge(prob_ready, ph + 1)
                    pe.wait_ge(proj_copied, len(tiles))
                for part, ci in enumerate(CENTRE_FIRST):
                    c = 12 * ph + 3 * s + part
                    if c >= 2:
                        pe.wait_ge(pv_ready, c - 1)
                    c0, c1, _ = columns(DIL[s], ci)
                    for j in range(4):
                        i0, i1 = row_offsets(s, j)
                        dims = lambda slot, row: [[slot, i1 - i0], [row, QR], [1, c1 - c0]]
                        o = view(ps, 1024 * (c % 2) + 64 * QR * j + W * i0 + c0, dims(W, 64))
                        m = view(prob, (ph * KK + 3 * ci + i0) * QP + c0, dims(QP, W))
                        last = mm(o, sel[:, j, s, :], m)
                    last.then_inc(spread_ready, 1)

            def restore(g):
                ph, first = g // 2, GB * (g % 2)
                if g % 2 == 0:
                    pe.wait_ge(added, ADDS * sum(POOL_SUMS[:ph + 1]))
                    if POOL_SUMS[ph] < ND:
                        pe.wait_ge(dve_added, ADDS * (ND - POOL_SUMS[ph]))
                if g == 0:
                    pe.wait_ge(shift_ready, PHASES)
                if g == 2:
                    pe.wait_ge(pv_ready, 12 * PHASES)
                for i in range(GB):
                    for s in range(ND):
                        last = mm(ps[32 * s:32 * s + 32, FIRST_BANK[g], N * i:N * i + N],
                                  ident[:, 32 * (first + i):32 * (first + i) + 32], acc[:, ph, s, :])
                last.then_inc(restored, 1)

            def group_stats(g):
                pe.wait_ge(stats_ready, g + 2)
                if g == 1:
                    pe.wait_ge(gexp_ready, 1)
                mm(ps[:, SECOND_BANK[g], 0:2 * GB].rearrange("p (i t) -> p i t", t=2), cs[:, C_GRP:C_GRP + P],
                   mv[:, group(g), :]).then_inc(gstats_ready, 1)

            def project_tokens(g):
                for i in range(GB):
                    pe.wait_ge(xn1_ready, GB * g + i + 1)
                    for t in range(2):
                        last = mm(ps[:, FIRST_BANK[g], N * i + P * t:N * i + P * t + P],
                                  xn1[:, g, i, P * t:P * t + P], wp[:, W_1T:W_1T + P])
                last.then_inc(pT_ready, 1)

            def attention(g):
                pe.wait_ge(pT_copied, g + 1)
                for i in range(GB):
                    for t in range(2):
                        for h in range(H1):
                            w = pT[:, g, 2 * i + t, HD1 * h:HD1 * h + HD1]
                            last = mm(ps[32 * h:32 * h + 32, SECOND_BANK[g], HD1 * i:HD1 * i + HD1], w, w,
                                      start=(t == 0), stop=(t == 1))
                last.then_inc(att_ready, 1)

            def fuse(g):
                pe.wait_ge(ablk_ready, g + 1)
                for i in range(GB):
                    last = mm(ps[:, FIRST_BANK[g], P * i:P * i + P], ablk[:, g, i, :], wp[:, W_PT:W_PT + P])
                last.then_inc(mT_ready, 1)

            def fuse_projection(g):
                pe.wait_ge(mT_copied, g + 1)
                for i in range(GB):
                    mm(ps[:, SECOND_BANK[g], P * i:P * i + P], wp[:, W_1:W_1 + P], mT[:, g, i, :])
                for i in range(GB):
                    last = mm(ps[:, FIRST_BANK[g], GB * P + i:GB * P + i + 1], mT[:, g, i, :], wp[:, W_B1:W_B1 + 1])
                last.then_inc(mwT_ready, 1)

            def finish(g):
                pe.wait_ge(mwT_copied, g + 1)
                for i in range(GB):
                    last = mm(ps[:, SECOND_BANK[g], N * i:N * i + N], mwT[:, g, i, :], xn1[:, g, i, :])
                last.then_inc(fin_ready, 1)

            steps = (restore, group_stats, project_tokens, attention, fuse, fuse_projection, finish)
            for n in range(8):
                project(n)
            gate_logits()
            for s in range(ND):
                sum_scores(0, s)
                project(8 + s)
            sum_scores(1, 0)
            pe.wait_ge(sel_loaded, 64)
            spread(0, 0)
            sum_scores(1, 1)
            spread(0, 1)
            sum_scores(1, 2)
            sum_scores(1, 3)
            spread(0, 2)
            spread(0, 3)
            for s in range(ND):
                spread(1, s)
                for step, g in PE_BETWEEN.get(s, ()):
                    steps[step](g)
            for step, g in order(PE_CHAIN, PE_BETWEEN):
                steps[step](g)


def kernel(**inputs):
    import numpy as np
    import concourse.bacc as bacc
    from concourse.bass_utils import run_bass_kernel_spmd

    def get(name):
        return np.asarray(inputs[name])

    w1, b1 = get("L1_conv_W_qkv"), get("L1_conv_b_qkv")
    wpack = np.concatenate([
        get("L0_conv_w_qkv").T, get("L0_conv_w_gate").T, w1, w1.T, get("L1_conv_W_proj").T, b1[:, None],
        get("L1_conv_b_proj")[:, None], np.broadcast_to(b1, (P, P)), np.broadcast_to(get("L0_conv_b_gate"), (P, ND))],
        axis=1)
    p = np.arange(P)
    score = np.arange(32)
    head_of = 2 * (p // CD) + p % CD // HD
    reduce_ = np.zeros((P, ND, 32), np.float32)
    for s in range(ND):
        reduce_[p, s, 8 * s + head_of] = 1
    consts = np.concatenate([
        np.eye(P, dtype=np.float32), (p[:, None] // GC == p // GC).astype(np.float32) / GC, reduce_.reshape(P, -1),
        (p[:, None] // HD1 == p // HD1).astype(np.float32),
        (p[:, None] % 32 // 8 == np.arange(ND)).astype(np.float32)], axis=1)
    selc = np.zeros((32, ND, P), np.float32)
    for s in range(ND):
        selc[:, s, :] = score[:, None] == 8 * s + head_of
    arrays = {"x_dram": np.ascontiguousarray(get("x").reshape(B, P, N)),
              "wpack_dram": np.ascontiguousarray(wpack), "consts_dram": np.ascontiguousarray(consts),
              "selc_dram": selc}
    nc = bacc.Bacc("TRN2", target_bir_lowering=False, num_devices=1)
    args = [nc.dram_tensor(n, a.shape, mybir.dt.from_np(a.dtype), kind="ExternalInput").ap() for n, a in arrays.items()]
    out = nc.dram_tensor("out_dram", (B, P, N), F32, kind="ExternalOutput").ap()
    build(nc, *args, out)
    r = run_bass_kernel_spmd(nc, [arrays], core_ids=[0])
    return r.results[0]["out_dram"].reshape(B, P, H, W)
```

```python
from contextlib import ExitStack

import concourse.bass as bass
from concourse import mybir

P = 128
B, H, W = 8, 16, 16
N = H * W
DIL = (1, 2, 4, 8)
ND = len(DIL)
CD = P // ND
HEADS = 2
HD = CD // HEADS
KK = 9
PHASES = 2
SLOTS = B // PHASES
QP = N // 4
QR = H // 4
GC = 4
H1 = 4
HD1 = P // H1
PAD = [d if d < 4 else 0 for d in DIL]
ROWS = [H + 2 * p for p in PAD]
EPS = 1e-5
SCALE0 = float(HD) ** -0.5
SCALE1 = float(N) ** -0.5
CENTRE_FIRST = (1, 0, 2)
GB = 2
GROUPS = B // GB
NORM_ON_ACT = (4, 6, 1, 3, 5, 7)
NORM_ON_DVE = (2, 3)
POOL_SUMS = (ND, 2)
RSQRT_AFTER = ((1, 0, 4), (1, 1, 0))


F32 = mybir.dt.float32
BF16 = mybir.dt.bfloat16
ALU = mybir.AluOpType
ACT = mybir.ActivationFunctionType
AX = mybir.AxisListType

W_QKV, W_GATE, W_1T, W_PT, W_B1, W_BP, W_BG, W_END = 0, 384, 388, 516, 644, 645, 646, 650
C_ID, C_GRP, C_RED, C_BLK, C_DIL, C_END = 0, 128, 256, 384, 512, 516


def columns(d, ci):
    co = (ci - 1) * d
    return max(0, -co), min(W, W - co), co


def pieces(s):
    d = DIL[s]
    if PAD[s]:
        return [(3, 0, 1, 0, 0, 0, d, H)]
    return [(1, 1, 0, 0, 0, 0, 0, H), (2, 0, 2, d, -d, 0, d, H - d)]


def row_offsets(s, j):
    if PAD[s]:
        return 0, 3
    return (0 if QR * j >= DIL[s] else 1), (3 if QR * j + DIL[s] < H else 2)


def additions(s):
    pairs = [(3 * ci + 1, 3 * ci + ri) for ci, ri in ((1, 0), (0, 0), (1, 2), (0, 2), (2, 0))]
    pairs += [(4, 1), (7, 8), (4, 7)]
    after = [None, None, 0, 1, None, 3, 4, 6]
    return [(t, a, f) for (t, a), f in zip(pairs, after)]


ADDS = len(additions(0))
ADD_NEEDS = (1, 2, 2, 2, 3, 3, 3, 3)


def valid_rows(s, ri):
    if PAD[s]:
        return 0, H
    ro = (ri - 1) * DIL[s]
    return max(0, -ro), min(H, H - ro)


def view(t, offset, dims, p0=0, parts=P):
    step = t[:].ap[0][0]
    return bass.AP(t, p0 * step + offset, [[step, parts]] + [list(x) for x in dims if x[1] > 1])


def build(nc, x, wpack, consts, selc, out):
    with ExitStack() as ctx:
        def sb(name, shape, dtype=F32):
            return ctx.enter_context(nc.sbuf_tensor(name, shape, dtype))

        def sem(name):
            return ctx.enter_context(nc.semaphore(name))

        xt = sb("xt", [P, B, N])
        xn = sb("xn", [P, B, N])
        wp = sb("wp", [P, W_END])
        cs = sb("cs", [P, C_END])
        sel = sb("sel", [P, 4, ND, P])
        q = sb("q", [P, ND, PHASES, N])
        k = [sb(f"k{s}", [P, PHASES, ROWS[s], W]) for s in range(ND)]
        v = [sb(f"v{s}", [P, PHASES, ROWS[s], W]) for s in range(ND)]
        qk = [sb(f"qk{s}", [P, KK, N]) for s in range(ND)]
        pv = [sb(f"pv{s}", [P, KK, N]) for s in range(ND)]
        acc = sb("acc", [P, PHASES, ND, N])
        shifted = sb("shifted", [P, KK, QP])
        expd = sb("expd", [P, KK, QP])
        prob = sb("prob", [P, PHASES, KK, QP])
        part = [sb(f"part{n}", [P, KK, QP], BF16) for n in range(3)]
        rest = sb("rest", [P, KK, QP])
        sel16 = sb("sel16", [P, 4, ND, P], BF16)
        smax = sb("smax", [P, QP])
        ssum = sb("ssum", [P, QP])
        srec = sb("srec", [P, QP])
        sums = sb("sums", [P, B, 2])
        sums1 = sb("sums1", [P, B, 2])
        gst = sb("gst", [P, B, 2])
        gsq = sb("gsq", [P, B])
        gvar = sb("gvar", [P, B])
        mhalf = sb("mhalf", [P, B])
        rstd = sb("rstd", [P, B])
        nbias = sb("nbias", [P, B])
        warm = sb("warm", [P, 1])
        pooled = sb("pooled", [P, B])
        pexp = sb("pexp", [P, PHASES, P])
        glog = sb("glog", [P, PHASES, ND])
        gsh = sb("gsh", [P, PHASES, ND])
        gex = sb("gex", [P, PHASES, ND])
        gpick = sb("gpick", [P, PHASES, ND])
        gmax = sb("gmax", [P, PHASES])
        minus = sb("minus", [P, 1])
        per_n = sb("per_n", [P, 1])
        signs = sb("signs", [P, 2])
        gtwo = sb("gtwo", [P, PHASES, ND // 2])
        gsum = sb("gsum", [P, PHASES])
        grec = sb("grec", [P, PHASES])
        gsel = sb("gsel", [P, PHASES])
        gate = sb("gate", [P, PHASES])
        x1 = sb("x1", [P, B, N])
        xn1 = sb("xn1", [P, GROUPS, GB, N])
        pT = sb("pT", [P, GROUPS, GB * 2, P])
        amax = sb("amax", [P, GROUPS, GB])
        ash = sb("ash", [P, GROUPS, GB, HD1])
        aex = sb("aex", [P, GROUPS, GB, HD1])
        asum = sb("asum", [P, GROUPS, GB])
        arec = sb("arec", [P, GROUPS, GB])
        ablk = sb("ablk", [P, GROUPS, GB, P])
        mT = sb("mT", [P, GROUPS, GB, P])
        p1 = sb("p1", [P, GROUPS, GB, N])

        ps = ctx.enter_context(nc.psum_tensor("ps", [P, 8, 512], F32))
        SC = (4, 6)
        ST = 7
        PROJ_BANKS = (0, 1, 2, 3, 6)
        IDLE_BANK = 5
        BANK = (4, 6, 0, 2)

        x_loaded = [sem(f"x_loaded{i}") for i in range(4)]
        w_loaded = sem("w_loaded")
        c_loaded = sem("c_loaded")
        grp_loaded = sem("grp_loaded")
        sel_zeroed = sem("sel_zeroed")
        sel_loaded = sem("sel_loaded")
        halo_zeroed = sem("halo_zeroed")
        dve_settled = sem("dve_settled")
        cells_set = sem("cells_set")
        sum_ready = sem("sum_ready")
        square_ready = sem("square_ready")
        gstats_ready = sem("gstats_ready")
        nbias_ready = sem("nbias_ready")
        var_ready = sem("var_ready")
        rstd_ready = sem("rstd_ready")
        pool_settled = sem("pool_settled")
        xn_ready = sem("xn_ready")
        xn_act_ready = sem("xn_act_ready")
        pexp_ready = sem("pexp_ready")
        glog_ready = sem("glog_ready")
        gate_ready = sem("gate_ready")
        gshift_ready = sem("gshift_ready")
        gexp_ready = sem("gexp_ready")
        proj_ready = sem("proj_ready")
        proj_copied = sem("proj_copied")
        qk_ready = sem("qk_ready")
        scores_ready = sem("scores_ready")
        shift_ready = sem("shift_ready")
        exp_ready = sem("exp_ready")
        prob_ready = sem("prob_ready")
        part_ready = [sem(f"part{n}_ready") for n in range(3)]
        rest_ready = sem("rest_ready")
        sel16_ready = sem("sel16_ready")
        spread_ready = sem("spread_ready")
        pv_ready = sem("pv_ready")
        added = sem("added")
        dve_added = sem("dve_added")
        restored = sem("restored")
        xn1_act_ready = sem("xn1_act_ready")
        xn1_ready = sem("xn1_ready")
        pT_ready = sem("pT_ready")
        pT_copied = sem("pT_copied")
        att_ready = sem("att_ready")
        ashift_ready = sem("ashift_ready")
        aexp_ready = sem("aexp_ready")
        ablk_ready = sem("ablk_ready")
        mT_ready = sem("mT_ready")
        mT_copied = sem("mT_copied")
        p1_ready = sem("p1_ready")
        p1_copied = sem("p1_copied")
        fin_ready = sem("fin_ready")
        out_ready = sem("out_ready")
        out_stored = sem("out_stored")

        ident = cs[:, C_ID:C_ID + P]

        def group(g):
            first = PHASES * GB * (g % 2) + g // 2
            return slice(first, first + PHASES * (GB - 1) + 1, PHASES)

        def batch(g, i):
            return group(g).start + PHASES * i

        tiles = []
        for ph in range(PHASES):
            tiles += [(kind, s, ph) for s in range(ND) for kind in (0, 1)] + [(2, s, ph) for s in range(ND)]

        def of_phase(ph):
            return slice(ph, B, PHASES)

        def operands(ph, s, n, target, slot):
            ci, ri = divmod(slot, 3)
            c0, c1, _ = columns(DIL[s], ci)
            r0, r1 = valid_rows(s, ri)

            def rect(t):
                return t.rearrange("p (r c) -> p r c", c=W)[:, r0:r1, c0:c1]

            o = rect(acc[:, ph, s, :] if target == 4 else pv[s][:, target, :])
            a = rect(pv[s][:, 4, :]) if n == 0 and PAD[s] else o
            return o, a, rect(pv[s][:, slot, :])

        block = ctx.enter_context(nc.Block())

        @block.sync
        def _(sp):
            xv = x.rearrange("b c n -> c b n")
            for i in range(4):
                first = B // 2 * (i % 2) + i // 2
                bs = slice(first, first + PHASES + 1, PHASES)
                sp.dma_start(xt[:, bs, :], xv[:, bs, :]).then_inc(x_loaded[i], 16)
            sp.dma_start(wp[:], wpack).then_inc(w_loaded, 16)
            sp.wait_ge(sel_zeroed, 1)
            for j in range(4):
                sp.dma_start(sel[32 * j:32 * j + 32, j, :, :], selc).then_inc(sel_loaded, 16)
            for n in range(B):
                b = batch(n // GB, n % GB)
                sp.wait_ge(out_ready, n + 1)
                sp.dma_start(out[b], x1[:, b, :]).then_inc(out_stored, 16)
            sp.wait_ge(out_stored, 16 * B)

        @block.gpsimd
        def _(pool):
            for cell, value in ((mhalf, -0.5), (minus, -1.0), (per_n, 1.0 / N)):
                nc.gpsimd.memset(cell[:], value).then_inc(cells_set, 1)
            nc.gpsimd.memset(sel[:], 0.0).then_inc(sel_zeroed, 1)
            for s in range(ND):
                if PAD[s]:
                    for t in (k[s], v[s]):
                        for r in (0, PAD[s] + H):
                            last = nc.gpsimd.memset(t[:, :, r:r + PAD[s], :], 0.0)
            last.then_inc(halo_zeroed, 1)
            pool_done = [0]

            def link(ins):
                pool_done[0] += 1
                ins.then_inc(pool_settled, 1)
                pool.wait_ge(pool_settled, pool_done[0])

            pool.wait_ge(cells_set, 3)

            def rsqrt(n, bs):
                pool.wait_ge(var_ready, n + 1)
                nc.gpsimd.tensor_tensor(rstd[:, bs], gvar[:, bs], mhalf[:, bs], ALU.pow).then_inc(rstd_ready, 1)

            for ph in range(PHASES):
                rsqrt(ph, of_phase(ph))

            pool.wait_ge(nbias_ready, PHASES)
            link(nc.gpsimd.tensor_tensor(pooled[:], sums[:, :, 0], view(per_n, 0, [[0, B]]), ALU.mult))
            link(nc.gpsimd.tensor_tensor(pooled[:], pooled[:], rstd[:], ALU.mult))
            link(nc.gpsimd.tensor_tensor(pooled[:], pooled[:], nbias[:], ALU.add))
            for ph in range(PHASES):
                dst = pexp[:, ph, :].rearrange("p (i j h) -> p i j h", j=SLOTS, h=HEADS)
                nc.gpsimd.tensor_copy(dst, view(pooled, ph, [[0, P // (SLOTS * HEADS)], [PHASES, SLOTS], [0, HEADS]])
                                      ).then_inc(pexp_ready, 1)
            pool.wait_ge(gexp_ready, 1)
            pool.wait_ge(c_loaded, 32)
            nc.gpsimd.tensor_tensor(gpick[:], gex[:], view(cs, C_DIL, [[0, PHASES], [1, ND]]), ALU.mult)
            link(nc.gpsimd.tensor_tensor(gtwo[:], gex[:, :, 0:2], gex[:, :, 2:4], ALU.add))
            link(nc.gpsimd.tensor_tensor(gsum[:], gtwo[:, :, 0], gtwo[:, :, 1], ALU.add))
            link(nc.gpsimd.tensor_tensor(grec[:], gsum[:], view(minus, 0, [[0, PHASES]]), ALU.pow))
            link(nc.gpsimd.tensor_tensor(gpick[:, :, 0:2], gpick[:, :, 0:2], gpick[:, :, 2:4], ALU.add))
            link(nc.gpsimd.tensor_tensor(gsel[:], gpick[:, :, 0], gpick[:, :, 1], ALU.add))
            nc.gpsimd.tensor_tensor(gate[:], gsel[:], grec[:], ALU.mult).then_inc(gate_ready, 1)

            base = 0
            for ph in range(PHASES):
                for s in range(POOL_SUMS[ph]):
                    for n, (target, slot, after) in enumerate(additions(s)):
                        chunk = 12 * ph + 3 * s + ADD_NEEDS[n]
                        if n == 0 or ADD_NEEDS[n] > ADD_NEEDS[n - 1]:
                            pool.wait_ge(pv_ready, chunk)
                        if after is not None:
                            pool.wait_ge(added, base + after + 1)
                        o, a, b = operands(ph, s, n, target, slot)
                        nc.gpsimd.tensor_tensor(o, a, b, ALU.add).then_inc(added, 1)
                        if (ph, s, n) in RSQRT_AFTER:
                            g = RSQRT_AFTER.index((ph, s, n))
                            rsqrt(PHASES + g, group(g))
                    base += ADDS
            for g in range(len(RSQRT_AFTER), GROUPS):
                rsqrt(PHASES + g, group(g))

        @block.scalar
        def _(act):
            act.dma_start(cs[:, C_GRP:C_GRP + P], consts[:, C_GRP:C_GRP + P]).then_inc(grp_loaded, 16)
            act.wait_ge(cells_set, 1)
            nc.scalar.activation(warm[:], mhalf[:, 0:1], ACT.Exp)

            def square_sum(n):
                ph, j = divmod(n, SLOTS)
                b = PHASES * j + ph
                act.wait_ge(x_loaded[n // 2], 16)
                nc.scalar.activation(xn1[:, b // GB, b % GB, :], xt[:, b, :], ACT.Square,
                                     accum_out=sums[:, b, 1:2]).then_inc(square_ready, 1)

            def load_consts():
                act.dma_start(cs[:, C_ID:C_ID + P], consts[:, C_ID:C_ID + P]).then_inc(c_loaded, 16)
                act.dma_start(cs[:, C_RED:C_END], consts[:, C_RED:C_END]).then_inc(c_loaded, 16)

            def first_norm(b):
                act.wait_ge(nbias_ready, b % PHASES + 1)
                nc.scalar.activation(xn[:, b, :], xt[:, b, :], ACT.Identity, bias=nbias[:, b:b + 1],
                                     scale=rstd[:, b:b + 1]).then_inc(xn_act_ready, 1)

            def copy_tile(n):
                kind, s, ph = tiles[n]
                if n == 0:
                    act.wait_ge(halo_zeroed, 1)
                act.wait_ge(proj_ready, n + 1)
                src = ps[:, PROJ_BANKS[n % len(PROJ_BANKS)], 0:N]
                if kind == 0:
                    nc.scalar.copy(q[:, s, ph, :], src).then_inc(proj_copied, 1)
                else:
                    dst = (k, v)[kind - 1][s][:, ph, PAD[s]:PAD[s] + H, :]
                    nc.scalar.copy(dst, src.rearrange("p (r c) -> p r c", c=W)).then_inc(proj_copied, 1)

            def gate_exp():
                act.wait_ge(gshift_ready, 1)
                nc.scalar.activation(gex[:], gsh[:], ACT.Exp).then_inc(gexp_ready, 1)

            def softmax_exp(ph):
                act.wait_ge(shift_ready, ph + 1)
                if ph:
                    act.wait_ge(prob_ready, ph)
                nc.scalar.activation(expd[:], shifted[:], ACT.Exp, scale=SCALE0).then_inc(exp_ready, 1)

            def copy_selection(s):
                act.wait_ge(sel_loaded, 64)
                nc.scalar.copy(sel16[:, :, s, :], sel[:, :, s, :]).then_inc(sel16_ready, 1)

            def first_part():
                act.wait_ge(prob_ready, PHASES)
                nc.scalar.copy(part[0][:], prob[:, PHASES - 1]).then_inc(part_ready[0], 1)

            def second_part():
                act.wait_ge(rest_ready, 1)
                nc.scalar.copy(part[1][:], rest[:]).then_inc(part_ready[1], 1)

            def squares(g):
                for i in range(GB):
                    b = batch(g, i)
                    act.wait_ge(sum_ready, B + GB * g + i + 1)
                    nc.scalar.activation(pT[:, g, 2 * i:2 * i + 2, :].rearrange("p t n -> p (t n)"), x1[:, b, :],
                                         ACT.Square, accum_out=sums1[:, b, 1:2]).then_inc(square_ready, 1)

            def norm(g, i):
                act.wait_ge(nbias_ready, PHASES + g + 1)
                b = batch(g, i)
                nc.scalar.activation(xn1[:, g, i, :], x1[:, b, :], ACT.Identity, bias=nbias[:, b:b + 1],
                                     scale=rstd[:, b:b + 1]).then_inc(xn1_act_ready, 1)

            def copy_projection(g, i):
                act.wait_ge(p1_ready, GB * g + i + 1)
                nc.scalar.activation(p1[:, g, i, :], ps[:, BANK[g] + i, 0:N], ACT.Identity,
                                     bias=wp[:, W_B1:W_B1 + 1]).then_inc(p1_copied, 1)

            def copy_pT(g, i):
                act.wait_ge(pT_ready, GB * g + i + 1)
                nc.scalar.copy(pT[:, g, 2 * i:2 * i + 2, :].rearrange("p a n -> p (a n)"),
                               ps[:, BANK[g] + i, 0:N]).then_inc(pT_copied, 1)

            def attention_exp(g):
                act.wait_ge(ashift_ready, g + 1)
                nc.scalar.activation(aex[:, g], ash[:, g], ACT.Exp, scale=SCALE1).then_inc(aexp_ready, 1)

            def copy_fused(g, i):
                act.wait_ge(mT_ready, GB * g + i + 1)
                nc.scalar.copy(mT[:, g, i, :], ps[:, BANK[g] + i, 0:P]).then_inc(mT_copied, 1)

            for n in range(8):
                square_sum(n)
            first_norm(4)
            first_norm(6)
            for n in range(4):
                copy_tile(n)
            first_norm(1)
            first_norm(3)
            copy_tile(4)
            load_consts()
            copy_tile(5)
            copy_tile(6)
            first_norm(5)
            first_norm(7)
            for n in range(7, 11):
                copy_tile(n)
            gate_exp()
            for n in range(11, 18):
                copy_tile(n)
            softmax_exp(0)
            for n in range(18, 24):
                copy_tile(n)
            softmax_exp(1)
            for n in range(1, 4):
                copy_selection(n)
            first_part()
            second_part()
            squares(0)
            squares(1)
            for i in range(2):
                norm(0, i)
            for i in range(2):
                norm(1, i)
            for i in range(2):
                copy_projection(0, i)
            copy_projection(1, 0)
            for i in range(2):
                copy_pT(0, i)
            copy_projection(1, 1)
            for i in range(2):
                copy_pT(1, i)
            attention_exp(0)
            squares(2)
            attention_exp(1)
            copy_fused(0, 0)
            squares(3)
            copy_fused(0, 1)
            copy_fused(1, 0)
            for i in range(2):
                copy_projection(2, i)
            copy_fused(1, 1)
            for i in range(2):
                copy_pT(2, i)
            for i in range(2):
                copy_projection(3, i)
            attention_exp(2)
            for i in range(2):
                copy_pT(3, i)
            copy_fused(2, 0)
            attention_exp(3)
            copy_fused(2, 1)
            for i in range(2):
                copy_fused(3, i)

        @block.vector
        def _(dve):
            settled = [0]

            def link(ins):
                settled[0] += 1
                ins.then_inc(dve_settled, 1)
                dve.wait_ge(dve_settled, settled[0])

            link(nc.vector.memset(signs[:, 0:1], -1.0))
            link(nc.vector.memset(signs[:, 1:2], 1.0))
            t = qk[0][:].rearrange("p (a i) (r c) -> p a (i r) c", i=3, c=W)
            nc.vector.memset(t[:, 0, :, 0:DIL[0]], 0.0)
            link(nc.vector.memset(t[:, 2, :, W - DIL[0]:W], 0.0))

            def norm_variance(n, bs, bank):
                dve.wait_ge(gstats_ready, n + 1)
                count = len(range(B)[bs])
                link(nc.vector.tensor_tensor(gst[:, bs, :], ps[:, bank, 0:2 * count].rearrange("p (b t) -> p b t", t=2),
                                             view(signs, 0, [[0, count], [1, 2]]), ALU.mult))
                link(nc.vector.tensor_tensor(gsq[:, bs], gst[:, bs, 0], gst[:, bs, 0], ALU.mult))
                nc.vector.scalar_tensor_tensor(out=gvar[:, bs], in0=gst[:, bs, 1], scalar=EPS, in1=gsq[:, bs],
                                               op0=ALU.add, op1=ALU.subtract).then_inc(var_ready, 1)

            def norm_bias(n, bs):
                dve.wait_ge(rstd_ready, n + 1)
                nc.vector.tensor_tensor(nbias[:, bs], gst[:, bs, 0], rstd[:, bs], ALU.mult).then_inc(nbias_ready, 1)

            def first_variance(ph):
                norm_variance(ph, of_phase(ph), ST)

            def first_norm_bias(ph):
                norm_bias(ph, of_phase(ph))

            def second_variance(g):
                norm_variance(PHASES + g, group(g), BANK[g])

            def second_norm_bias(g):
                norm_bias(PHASES + g, group(g))

            def channel_sum(n):
                ph, j = divmod(n, SLOTS)
                b = PHASES * j + ph
                dve.wait_ge(x_loaded[n // 2], 16)
                nc.vector.tensor_reduce(sums[:, b, 0:1], xt[:, b, :], AX.X, ALU.add).then_inc(sum_ready, 1)

            def first_norm(b):
                dve.wait_ge(nbias_ready, b % PHASES + 1)
                nc.vector.tensor_scalar(xn[:, b, :], xt[:, b, :], rstd[:, b:b + 1], nbias[:, b:b + 1],
                                        ALU.mult, ALU.add).then_inc(xn_ready, 1)

            def gate_shift():
                dve.wait_ge(glog_ready, 1)
                link(nc.vector.tensor_tensor(glog[:], ps[:, ST, 32:32 + PHASES * ND].rearrange("p (h s) -> p h s", s=ND),
                                             view(wp, W_BG, [[0, PHASES], [1, ND]]), ALU.add))
                link(nc.vector.tensor_reduce(gmax[:], glog[:], AX.X, ALU.max))
                nc.vector.tensor_tensor(gsh[:], glog[:], view(gmax, 0, [[1, PHASES], [0, ND]]),
                                        ALU.subtract).then_inc(gshift_ready, 1)

            def multiply_qk(ph, s, ci):
                if ci == 0:
                    dve.wait_ge(proj_copied, tiles.index((1, s, ph)) + 1)
                if ph and ci == 0:
                    dve.wait_ge(scores_ready, s + 1)
                c0, c1, co = columns(DIL[s], ci)
                for n, ri, dri, r0, dr, a0, da, rows in pieces(s):
                    o = view(qk[s], (3 * ci + ri) * N + r0 * W + c0, [[dri * N + dr * W, n], [W, rows], [1, c1 - c0]])
                    a = view(q, (s * PHASES + ph) * N + r0 * W + c0, [[dr * W, n], [W, rows], [1, c1 - c0]])
                    b = view(k[s], (ph * ROWS[s] + a0) * W + c0 + co, [[da * W, n], [W, rows], [1, c1 - c0]])
                    last = nc.vector.tensor_tensor(o, a, b, ALU.mult)
                if ci == 2:
                    last.then_inc(qk_ready, 1)

            def softmax_shift(ph):
                dve.wait_ge(scores_ready, ND * (ph + 1))
                link(nc.vector.tensor_reduce(smax[:], view(ps, 512 * SC[ph], [[1, QP], [256, 3], [QP, 3]]), AX.XY, ALU.max))
                if ph:
                    dve.wait_ge(exp_ready, ph)
                nc.vector.tensor_tensor(shifted[:].rearrange("p (c r) n -> p c r n", r=3),
                                        view(ps, 512 * SC[ph], [[256, 3], [QP, 3], [1, QP]]),
                                        view(smax, 0, [[0, 3], [0, 3], [1, QP]]), ALU.subtract).then_inc(shift_ready, 1)

            def softmax_divide(ph):
                dve.wait_ge(exp_ready, ph + 1)
                link(nc.vector.tensor_reduce(ssum[:], view(expd, 0, [[1, QP], [QP, KK]]), AX.X, ALU.add))
                link(nc.vector.reciprocal(srec[:], ssum[:]))
                dve.wait_ge(gate_ready, 1)
                nc.vector.scalar_tensor_tensor(out=prob[:, ph, :, :], in0=expd[:], scalar=gate[:, ph:ph + 1],
                                               in1=view(srec, 0, [[0, KK], [1, QP]]), op0=ALU.mult, op1=ALU.mult
                                               ).then_inc(prob_ready, 1)

            def split_rest():
                dve.wait_ge(part_ready[0], 1)
                nc.vector.tensor_tensor(rest[:], prob[:, PHASES - 1], part[0][:], ALU.subtract).then_inc(rest_ready, 1)

            def third_part():
                dve.wait_ge(part_ready[1], 1)
                nc.vector.tensor_tensor(part[2][:], rest[:], part[1][:], ALU.subtract).then_inc(part_ready[2], 1)

            def multiply_pv(ph, s, chunk):
                ci = CENTRE_FIRST[chunk]
                c = 12 * ph + 3 * s + chunk
                if chunk == 0:
                    dve.wait_ge(proj_copied, tiles.index((2, s, ph)) + 1)
                dve.wait_ge(spread_ready, c + 1)
                if ph and chunk == 0:
                    dve.wait_ge(added, ADDS * (s + 1))
                c0, c1, co = columns(DIL[s], ci)
                nc_ = c1 - c0
                for n, ri, dri, r0, dr, a0, da, rows in pieces(s):
                    o = view(pv[s], (3 * ci + ri) * N + r0 * W + c0, [[dri * N + dr * W, n], [W, rows], [1, nc_]])
                    if ci == 1 and n == 1:
                        o = view(acc, (ph * ND + s) * N, [[W, rows], [1, nc_]])
                    a = view(ps, 1024 * (c % 2) + 64 * r0 + W * ri + c0, [[W * dri + 64 * dr, n], [64, rows], [1, nc_]])
                    b = view(v[s], (ph * ROWS[s] + a0) * W + c0 + co, [[da * W, n], [W, rows], [1, nc_]])
                    last = nc.vector.tensor_tensor(o, a, b, ALU.mult)
                last.then_inc(pv_ready, 1)

            def add_neighbours(ph, s):
                done = ADDS * (s - POOL_SUMS[ph])
                for n, (target, slot, after) in enumerate(additions(s)):
                    if n == 0 or ADD_NEEDS[n] > ADD_NEEDS[n - 1]:
                        dve.wait_ge(pv_ready, 12 * ph + 3 * s + ADD_NEEDS[n])
                    if after is not None:
                        dve.wait_ge(dve_added, done + after + 1)
                    o, a, b = operands(ph, s, n, target, slot)
                    nc.vector.tensor_tensor(o, a, b, ALU.add).then_inc(dve_added, 1)

            def first_residual(g):
                for i in range(GB):
                    dve.wait_ge(restored, GB * g + i + 1)
                    b = batch(g, i)
                    nc.vector.scalar_tensor_tensor(out=x1[:, b, :], in0=ps[:, BANK[g] + i, 0:N], scalar=1.0,
                                                   in1=xt[:, b, :], op0=ALU.mult, op1=ALU.add,
                                                   accum_out=sums1[:, b, 0:1]).then_inc(sum_ready, 1)

            def attention_shift(g):
                dve.wait_ge(att_ready, g + 1)
                att = ps[:, BANK[g]:BANK[g] + GB, 0:HD1]
                link(nc.vector.tensor_reduce(amax[:, g], att, AX.X, ALU.max))
                nc.vector.tensor_tensor(ash[:, g], att, view(amax, GB * g, [[1, GB], [0, HD1]]),
                                        ALU.subtract).then_inc(ashift_ready, 1)

            def attention_divide(g):
                dve.wait_ge(aexp_ready, g + 1)
                link(nc.vector.tensor_reduce(asum[:, g], aex[:, g], AX.X, ALU.add))
                link(nc.vector.reciprocal(arec[:, g], asum[:, g]))
                for i in range(GB):
                    nc.vector.scalar_tensor_tensor(out=ablk[:, g, i, :].rearrange("p (h e) -> p h e", h=H1),
                                                   in0=view(aex, (GB * g + i) * HD1, [[0, H1], [1, HD1]]),
                                                   scalar=arec[:, g, i:i + 1], in1=view(cs, C_BLK, [[HD1, H1], [1, HD1]]),
                                                   op0=ALU.mult, op1=ALU.mult).then_inc(ablk_ready, 1)

            def second_residual(g, i):
                dve.wait_ge(fin_ready, GB * g + i + 1)
                b = batch(g, i)
                nc.vector.scalar_tensor_tensor(out=x1[:, b, :], in0=ps[:, BANK[g] + i, 0:N],
                                               scalar=wp[:, W_BP:W_BP + 1], in1=x1[:, b, :], op0=ALU.add,
                                               op1=ALU.add).then_inc(out_ready, 1)

            def norm(g, i):
                b = batch(g, i)
                dve.wait_ge(nbias_ready, PHASES + g + 1)
                nc.vector.tensor_scalar(xn1[:, g, i, :], x1[:, b, :], rstd[:, b:b + 1], nbias[:, b:b + 1],
                                        ALU.mult, ALU.add).then_inc(xn1_ready, 1)

            for n in range(5):
                channel_sum(n)
            first_variance(0)
            for n in range(5, 8):
                channel_sum(n)
            first_norm_bias(0)
            first_norm(0)
            first_norm(2)
            first_variance(1)
            first_norm_bias(1)
            for i in range(3):
                multiply_qk(0, 0, i)
            for i in range(3):
                multiply_qk(0, 1, i)
            for i in range(2):
                multiply_qk(0, 2, i)
            gate_shift()
            multiply_qk(0, 2, 2)
            for i in range(3):
                multiply_qk(0, 3, i)
            for i in range(2):
                multiply_qk(1, 0, i)
            softmax_shift(0)
            multiply_qk(1, 0, 2)
            multiply_qk(1, 1, 0)
            softmax_divide(0)
            for i in range(1, 3):
                multiply_qk(1, 1, i)
            multiply_qk(1, 2, 0)
            for i in range(3):
                multiply_pv(0, 0, i)
            for i in range(1, 3):
                multiply_qk(1, 2, i)
            for i in range(2):
                multiply_pv(0, 1, i)
            for i in range(3):
                multiply_qk(1, 3, i)
            multiply_pv(0, 1, 2)
            for i in range(3):
                multiply_pv(0, 2, i)
            softmax_shift(1)
            for i in range(2):
                multiply_pv(0, 3, i)
            softmax_divide(1)
            multiply_pv(0, 3, 2)
            split_rest()
            for i in range(2):
                multiply_pv(1, 0, i)
            third_part()
            first_residual(0)
            multiply_pv(1, 0, 2)
            multiply_pv(1, 1, 0)
            second_variance(0)
            first_residual(1)
            for i in range(1, 3):
                multiply_pv(1, 1, i)
            second_variance(1)
            for i in range(2):
                multiply_pv(1, 2, i)
            second_norm_bias(0)
            second_norm_bias(1)
            multiply_pv(1, 2, 2)
            multiply_pv(1, 3, 0)
            add_neighbours(1, 2)
            for i in range(1, 3):
                multiply_pv(1, 3, i)
            add_neighbours(1, 3)
            attention_shift(0)
            attention_shift(1)
            first_residual(2)
            attention_divide(0)
            first_residual(3)
            second_variance(2)
            attention_divide(1)
            second_norm_bias(2)
            second_variance(3)
            for i in range(2):
                norm(2, i)
            second_norm_bias(3)
            for i in range(2):
                norm(3, i)
            for i in range(2):
                second_residual(0, i)
            attention_shift(2)
            attention_divide(2)
            attention_shift(3)
            second_residual(1, 0)
            attention_divide(3)
            second_residual(1, 1)
            for i in range(2):
                second_residual(2, i)
            for i in range(2):
                second_residual(3, i)

        @block.tensor
        def _(pe):
            def mm(o, w, m, start=True, stop=True):
                return nc.tensor.matmul(o, w, m, start=start, stop=stop)

            def keep_clock(n, shifted=0):
                if shifted:
                    pe.wait_ge(shift_ready, shifted)
                for _ in range(n):
                    mm(ps[:, IDLE_BANK, 0:P], xt[:, 0, 0:P], xt[:, 0, 0:P])

            def first_stats(ph):
                if ph == 0:
                    pe.wait_ge(grp_loaded, 16)
                else:
                    pe.wait_ge(var_ready, ph)
                pe.wait_ge(sum_ready, SLOTS * (ph + 1))
                pe.wait_ge(square_ready, SLOTS * (ph + 1))
                mm(ps[:, ST, 0:2 * SLOTS].rearrange("p (j t) -> p j t", t=2), cs[:, C_GRP:C_GRP + P],
                   sums[:, of_phase(ph), :]).then_inc(gstats_ready, 1)

            def project(n):
                kind, s, ph = tiles[n]
                if n == 0:
                    pe.wait_ge(w_loaded, 16)
                bank = PROJ_BANKS[n % len(PROJ_BANKS)]
                if n >= len(PROJ_BANKS):
                    pe.wait_ge(proj_copied, n - len(PROJ_BANKS) + 1)
                w0 = W_QKV + P * kind + CD * s
                for j in range(SLOTS):
                    b = PHASES * j + ph
                    if n % (3 * ND) == 0:
                        every = [PHASES * i + h for h in range(PHASES) for i in range(SLOTS)]
                        same = [x for x in every if (x in NORM_ON_ACT) == (b in NORM_ON_ACT)]
                        pe.wait_ge(xn_act_ready if b in NORM_ON_ACT else xn_ready, same.index(b) + 1)
                    last = mm(ps[32 * j:32 * j + 32, bank, 0:N], wp[:, w0:w0 + CD], xn[:, b, :])
                last.then_inc(proj_ready, 1)

            def gate_logits():
                pe.wait_ge(pexp_ready, PHASES)
                pe.wait_ge(var_ready, PHASES)
                for ph in range(PHASES):
                    last = mm(ps[:, ST, 32 + ND * ph:32 + ND * ph + ND], pexp[:, ph, :], wp[:, W_GATE:W_GATE + ND])
                last.then_inc(glog_ready, 1)

            def sum_scores(ph, s):
                if s == 0 and ph:
                    pe.wait_ge(proj_copied, len(tiles))
                    pe.wait_ge(gshift_ready, 1)
                if s == 0 and ph == 0:
                    pe.wait_ge(c_loaded, 32)
                pe.wait_ge(qk_ready, ND * ph + s + 1)
                w = cs[:, C_RED + 32 * s:C_RED + 32 * s + 32]
                for ci, n in ((0, 2), (2, 1)) if s == 0 else ((0, 1), (1, 1), (2, 1)):
                    c0, c1, _ = columns(DIL[s], ci) if s else (0, W, 0)
                    for j in range(4):
                        i0, i1 = row_offsets(s, j)

                        def dims(offset, slot):
                            if s == 0:
                                return [[offset, n], [slot, 3], [1, QP]]
                            return [[slot, i1 - i0], [W, QR], [1, c1 - c0]]

                        o = view(ps, 512 * SC[ph] + 256 * ci + QP * i0 + c0, dims(256, QP), 32 * j, 32)
                        m = view(qk[s], (3 * ci + i0) * N + QP * j + c0, dims(3 * N, N))
                        last = mm(o, w, m, start=(s == 0), stop=(s == ND - 1 and ci > 0))
                last.then_inc(scores_ready, 1)

            def spread(ph, s, chunk):
                ci = CENTRE_FIRST[chunk]
                c = 12 * ph + 3 * s + chunk
                if c % 12 == 0:
                    pe.wait_ge(prob_ready, ph + 1)
                if c == 0:
                    pe.wait_ge(sel_loaded, 64)
                    pe.wait_ge(proj_copied, len(tiles))
                if c >= 2:
                    pe.wait_ge(pv_ready, c - 1)
                split = ph == PHASES - 1 and s > 0
                if split and s == 1 and chunk == 0:
                    pe.wait_ge(sel16_ready, ND - 1)
                    for n in range(3):
                        pe.wait_ge(part_ready[n], 1)
                c0, c1, _ = columns(DIL[s], ci)
                for j in range(4):
                    i0, i1 = row_offsets(s, j)
                    dims = lambda slot, row: [[slot, i1 - i0], [row, QR], [1, c1 - c0]]
                    o = view(ps, 1024 * (c % 2) + 64 * QR * j + W * i0 + c0, dims(W, 64))
                    for n in range(3 if split else 1):
                        if split:
                            w, m = sel16, view(part[n], (3 * ci + i0) * QP + c0, dims(QP, W))
                        else:
                            w, m = sel, view(prob, (ph * KK + 3 * ci + i0) * QP + c0, dims(QP, W))
                        last = mm(o, w[:, j, s, :], m, start=(n == 0), stop=(n == 2 or not split))
                last.then_inc(spread_ready, 1)

            def restore(g):
                ph, first = g // 2, GB * (g % 2)
                if g % 2 == 0:
                    pe.wait_ge(added, ADDS * sum(POOL_SUMS[:ph + 1]))
                    if POOL_SUMS[ph] < ND:
                        pe.wait_ge(dve_added, ADDS * (ND - POOL_SUMS[ph]))
                if ph == 0:
                    pe.wait_ge(shift_ready, g + 1)
                if g == 2:
                    pe.wait_ge(pv_ready, 12 * PHASES)
                for i in range(GB):
                    for s in range(ND):
                        last = mm(ps[32 * s:32 * s + 32, BANK[g] + i, 0:N],
                                  ident[:, 32 * (first + i):32 * (first + i) + 32], acc[:, ph, s, :])
                    last.then_inc(restored, 1)

            def group_stats(g):
                pe.wait_ge(sum_ready, B + GB * (g + 1))
                pe.wait_ge(square_ready, B + GB * (g + 1))
                mm(ps[:, BANK[g], 0:2 * GB].rearrange("p (i t) -> p i t", t=2), cs[:, C_GRP:C_GRP + P],
                   sums1[:, group(g), :]).then_inc(gstats_ready, 1)

            def project_second(g, i):
                if g in NORM_ON_DVE:
                    pe.wait_ge(xn1_ready, GB * (g - NORM_ON_DVE[0]) + i + 1)
                else:
                    pe.wait_ge(xn1_act_ready, GB * g + i + 1)
                mm(ps[:, BANK[g] + i, 0:N], wp[:, W_1T:W_1T + P], xn1[:, g, i, :]).then_inc(p1_ready, 1)

            def transpose(g, i):
                pe.wait_ge(p1_copied, GB * g + i + 1)
                for t in range(2):
                    last = nc.tensor.transpose(ps[:, BANK[g] + i, P * t:P * t + P],
                                               p1[:, g, i, P * t:P * t + P], ident)
                last.then_inc(pT_ready, 1)

            def attention(g):
                for i in range(GB):
                    pe.wait_ge(pT_copied, GB * g + i + 1)
                    for t in range(2):
                        for h in range(H1):
                            w = pT[:, g, 2 * i + t, HD1 * h:HD1 * h + HD1]
                            last = mm(ps[32 * h:32 * h + 32, BANK[g] + i, 0:HD1], w, w,
                                      start=(t == 0), stop=(t == 1))
                last.then_inc(att_ready, 1)

            def fuse(g, i):
                pe.wait_ge(ablk_ready, GB * g + i + 1)
                mm(ps[:, BANK[g] + i, 0:P], ablk[:, g, i, :], wp[:, W_PT:W_PT + P]).then_inc(mT_ready, 1)

            def finish(g, i):
                pe.wait_ge(mT_copied, GB * g + i + 1)
                mm(ps[:, BANK[g] + i, 0:N], mT[:, g, i, :], p1[:, g, i, :]).then_inc(fin_ready, 1)

            pe.wait_ge(x_loaded[0], 16)
            keep_clock(4)
            first_stats(0)
            keep_clock(5)
            first_stats(1)
            for n in range(11):
                project(n)
            gate_logits()
            sum_scores(0, 0)
            project(11)
            project(12)
            sum_scores(0, 1)
            project(13)
            project(14)
            for i in range(2, 4):
                sum_scores(0, i)
            for n in range(15, 24):
                project(n)
            sum_scores(1, 0)
            for i in range(3):
                spread(0, 0, i)
            for i in range(2):
                spread(0, 1, i)
            sum_scores(1, 1)
            spread(0, 1, 2)
            spread(0, 2, 0)
            sum_scores(1, 2)
            for i in range(1, 3):
                spread(0, 2, i)
            sum_scores(1, 3)
            for i in range(3):
                spread(0, 3, i)
            keep_clock(2, 1)
            keep_clock(3, 1)
            for i in range(2):
                spread(1, 0, i)
            restore(0)
            spread(1, 0, 2)
            spread(1, 1, 0)
            group_stats(0)
            restore(1)
            for i in range(1, 3):
                spread(1, 1, i)
            group_stats(1)
            for i in range(3):
                spread(1, 2, i)
            spread(1, 3, 0)
            for i in range(2):
                project_second(0, i)
            for i in range(2):
                project_second(1, i)
            for i in range(2):
                transpose(0, i)
            for i in range(1, 3):
                spread(1, 3, i)
            transpose(1, 0)
            attention(0)
            transpose(1, 1)
            attention(1)
            restore(2)
            restore(3)
            fuse(0, 0)
            group_stats(2)
            finish(0, 0)
            group_stats(3)
            fuse(0, 1)
            for i in range(2):
                fuse(1, i)
            finish(0, 1)
            for i in range(2):
                project_second(2, i)
            project_second(3, 0)
            for i in range(2):
                transpose(2, i)
            project_second(3, 1)
            attention(2)
            for i in range(2):
                transpose(3, i)
            finish(1, 0)
            attention(3)
            for i in range(2):
                fuse(2, i)
            finish(1, 1)
            for i in range(2):
                finish(2, i)
            for i in range(2):
                fuse(3, i)
            for i in range(2):
                finish(3, i)


def kernel(**inputs):
    import numpy as np
    import concourse.bacc as bacc
    from concourse.bass_utils import run_bass_kernel_spmd

    def get(name):
        return np.asarray(inputs[name])

    wpack = np.concatenate([
        get("L0_conv_w_qkv").T, get("L0_conv_w_gate").T, get("L1_conv_W_qkv").T, get("L1_conv_W_proj").T,
        get("L1_conv_b_qkv")[:, None], get("L1_conv_b_proj")[:, None],
        np.broadcast_to(get("L0_conv_b_gate"), (P, ND))], axis=1)
    p = np.arange(P)
    score = np.arange(32)
    head_of = 2 * (p // CD) + p % CD // HD
    reduce_ = np.zeros((P, ND, 32), np.float32)
    for s in range(ND):
        reduce_[p, s, 8 * s + head_of] = 1
    consts = np.concatenate([
        np.eye(P, dtype=np.float32), (p[:, None] // GC == p // GC).astype(np.float32) / (GC * N), reduce_.reshape(P, -1),
        (p[:, None] // HD1 == p // HD1).astype(np.float32),
        (p[:, None] % 32 // 8 == np.arange(ND)).astype(np.float32)], axis=1)
    selc = np.zeros((32, ND, P), np.float32)
    for s in range(ND):
        selc[:, s, :] = score[:, None] == 8 * s + head_of
    arrays = {"x_dram": np.ascontiguousarray(get("x").reshape(B, P, N)),
              "wpack_dram": np.ascontiguousarray(wpack), "consts_dram": np.ascontiguousarray(consts),
              "selc_dram": selc}
    nc = bacc.Bacc("TRN2", target_bir_lowering=False, num_devices=1)
    args = [nc.dram_tensor(n, a.shape, mybir.dt.from_np(a.dtype), kind="ExternalInput").ap() for n, a in arrays.items()]
    out = nc.dram_tensor("out_dram", (B, P, N), F32, kind="ExternalOutput").ap()
    build(nc, *args, out)
    r = run_bass_kernel_spmd(nc, [arrays], core_ids=[0])
    return r.results[0]["out_dram"].reshape(B, P, H, W)
```
